# Optimizing a Trainium2 kernel written in Bass

```python
import numpy as np
import jax
import jax.numpy as jnp

def _softmax(x, axis=-1):
    return jax.nn.softmax(x, axis=axis)

def _gelu(x):
    return jax.nn.gelu(x, approximate=True)

def _silu(x):
    return jax.nn.silu(x)

def _sigmoid(x):
    return jax.nn.sigmoid(x)

def _layernorm(x, axis=-1, eps=1e-05):
    m = jnp.mean(x, axis=axis, keepdims=True)
    v = jnp.var(x, axis=axis, keepdims=True)
    return (x - m) / jnp.sqrt(v + eps)

def _scatter_add(tgt, idx, src, axis=0):
    return tgt.at[idx].add(src)

def _segment_sum(src, seg, n):
    return jax.ops.segment_sum(src, seg, n)
kernel_name = 'mk_macaron_d1_jaxref_r8_122c66'

def setup_inputs(seed: int=0):
    np.random.seed(seed)
    _w = jnp.asarray

    def _L0_attn_setup():
        import jax, jax.numpy as jnp
        import numpy as np
        NUM_Q_HEADS = 32
        NUM_KV_GROUPS = 8
        HEAD_SIZE = 128
        ROPE_THETA = 10000.0

        def _rope_cos_sin(T, dim, dtype=jnp.float32):
            freqs = 1.0 / ROPE_THETA ** (jnp.arange(0, dim, 2, dtype=jnp.float32) / dim)
            angle = jnp.arange(T, dtype=jnp.float32)[:, None] * freqs[None, :]
            return (jnp.cos(angle).astype(dtype), jnp.sin(angle).astype(dtype))

        def _apply_rope(x, cos, sin):
            xr = x[..., 0::2]
            xi = x[..., 1::2]
            or_ = xr * cos - xi * sin
            oi_ = xr * sin + xi * cos
            out = jnp.stack([or_, oi_], axis=-1)
            return out.reshape(x.shape)
        key = jax.random.key(seed)
        ks = jax.random.split(key, 5)
        B, T, C = (2, 128, 512)
        H, G, D = (NUM_Q_HEADS, NUM_KV_GROUPS, HEAD_SIZE)
        s = 1.0 / np.sqrt(C)
        return {'x': jax.random.normal(ks[0], (B, T, C), dtype=jnp.float32), 'Wq': jax.random.normal(ks[1], (C, H * D), dtype=jnp.float32) * s, 'Wk': jax.random.normal(ks[2], (C, G * D), dtype=jnp.float32) * s, 'Wv': jax.random.normal(ks[3], (C, G * D), dtype=jnp.float32) * s, 'Wo': jax.random.normal(ks[4], (H * D, C), dtype=jnp.float32) * (1.0 / np.sqrt(H * D)), 'bo': jnp.zeros((C,), dtype=jnp.float32)}
    _L0_attn_in = _L0_attn_setup()

    def _L0_ffn_setup():
        import jax, jax.numpy as jnp
        import numpy as np
        HID, BOT, RDIM, NSLOT, K, VB = (512, 64, 48, 128, 8, 32)
        TAU_LOW, TAU_HIGH, EARLY_EXIT = (0.5, 2.0, 0.05)

        def _uncertainty(h, Wu1, bu1, Wu2, bu2):
            var = jnp.var(h, axis=-1)
            log_var = jnp.log1p(var)
            norm_var = log_var / (jnp.mean(log_var) + 1e-06)
            learned = (jax.nn.gelu(h @ Wu1.T + bu1) @ Wu2.T + bu2)[..., 0]
            return jnp.clip(norm_var * 0.5 + jax.nn.sigmoid(learned) * 2.5, 0.0, 5.0)
        key = jax.random.key(seed)
        ks = jax.random.split(key, 12)
        B, S = (2, 256)
        return {'hidden_states': jax.random.normal(ks[0], (B, S, HID), dtype=jnp.float32), 'Wq': jax.random.normal(ks[1], (BOT, HID), dtype=jnp.float32) / np.sqrt(HID), 'Wr': jax.random.normal(ks[2], (RDIM, BOT), dtype=jnp.float32) / np.sqrt(BOT), 'aux_keys': jax.random.normal(ks[3], (NSLOT, BOT), dtype=jnp.float32) * 0.01, 'aux_values': jax.random.normal(ks[4], (NSLOT, HID), dtype=jnp.float32) * 0.02, 'Wvd': jax.random.normal(ks[5], (VB, HID), dtype=jnp.float32) * 0.1 / np.sqrt(HID), 'Wvu': jax.random.normal(ks[6], (HID, VB), dtype=jnp.float32) * 0.1 / np.sqrt(VB), 'Wu1': jax.random.normal(ks[7], (HID // 4, HID), dtype=jnp.float32) / np.sqrt(HID), 'bu1': jnp.zeros((HID // 4,), dtype=jnp.float32), 'Wu2': jax.random.normal(ks[8], (1, HID // 4), dtype=jnp.float32) * 0.01, 'bu2': jnp.zeros((1,), dtype=jnp.float32), 'gate_w1': jnp.float32(0.5), 'gate_bias': jnp.float32(-1.0), 'log_rel': jnp.zeros((NSLOT,), dtype=jnp.float32)}
    _L0_ffn_in = _L0_ffn_setup()
    _d = {'L0_attn_x': _L0_attn_in['x'], 'L0_attn_Wq': _L0_attn_in['Wq'], 'L0_attn_Wk': _L0_attn_in['Wk'], 'L0_attn_Wv': _L0_attn_in['Wv'], 'L0_attn_Wo': _L0_attn_in['Wo'], 'L0_attn_bo': _L0_attn_in['bo'], 'L0_ffn_Wq': _L0_ffn_in['Wq'], 'L0_ffn_Wr': _L0_ffn_in['Wr'], 'L0_ffn_aux_keys': _L0_ffn_in['aux_keys'], 'L0_ffn_aux_values': _L0_ffn_in['aux_values'], 'L0_ffn_Wvd': _L0_ffn_in['Wvd'], 'L0_ffn_Wvu': _L0_ffn_in['Wvu'], 'L0_ffn_Wu1': _L0_ffn_in['Wu1'], 'L0_ffn_bu1': _L0_ffn_in['bu1'], 'L0_ffn_Wu2': _L0_ffn_in['Wu2'], 'L0_ffn_bu2': _L0_ffn_in['bu2'], 'L0_ffn_gate_w1': _L0_ffn_in['gate_w1'], 'L0_ffn_gate_bias': _L0_ffn_in['gate_bias'], 'L0_ffn_log_rel': _L0_ffn_in['log_rel']}
    _x0 = _d['L0_attn_x']
    _d['L0_attn_x'] = jax.random.normal(jax.random.fold_in(jax.random.key(seed), 1), (4, 512, 512), dtype=_x0.dtype)
    del _x0
    return _d

def reference(L0_attn_x, L0_attn_Wq, L0_attn_Wk, L0_attn_Wv, L0_attn_Wo, L0_attn_bo, L0_ffn_Wq, L0_ffn_Wr, L0_ffn_aux_keys, L0_ffn_aux_values, L0_ffn_Wvd, L0_ffn_Wvu, L0_ffn_Wu1, L0_ffn_bu1, L0_ffn_Wu2, L0_ffn_bu2, L0_ffn_gate_w1, L0_ffn_gate_bias, L0_ffn_log_rel):

    def _L0_attn_ref(x, Wq, Wk, Wv, Wo, bo):
        import jax, jax.numpy as jnp
        import numpy as np
        NUM_Q_HEADS = 32
        NUM_KV_GROUPS = 8
        HEAD_SIZE = 128
        ROPE_THETA = 10000.0

        def _rope_cos_sin(T, dim, dtype=jnp.float32):
            freqs = 1.0 / ROPE_THETA ** (jnp.arange(0, dim, 2, dtype=jnp.float32) / dim)
            angle = jnp.arange(T, dtype=jnp.float32)[:, None] * freqs[None, :]
            return (jnp.cos(angle).astype(dtype), jnp.sin(angle).astype(dtype))

        def _apply_rope(x, cos, sin):
            xr = x[..., 0::2]
            xi = x[..., 1::2]
            or_ = xr * cos - xi * sin
            oi_ = xr * sin + xi * cos
            out = jnp.stack([or_, oi_], axis=-1)
            return out.reshape(x.shape)
        B, T, C = x.shape
        H, G, D = (NUM_Q_HEADS, NUM_KV_GROUPS, HEAD_SIZE)
        rep = H // G
        q = (x @ Wq).reshape(B, T, H, D).transpose(0, 2, 1, 3)
        k = (x @ Wk).reshape(B, T, G, D).transpose(0, 2, 1, 3)
        v = (x @ Wv).reshape(B, T, G, D).transpose(0, 2, 1, 3)
        cos, sin = _rope_cos_sin(T, D)
        q = _apply_rope(q, cos, sin)
        k = _apply_rope(k, cos, sin)
        qg = q.reshape(B, G, rep, T, D)
        scores = jnp.einsum('bgrtd,bgsd->bgrts', qg, k) * D ** (-0.5)
        causal = jnp.tril(jnp.ones((T, T), dtype=bool))
        scores = jnp.where(causal, scores, -jnp.inf)
        probs = jax.nn.softmax(scores, axis=-1)
        out = jnp.einsum('bgrts,bgsd->bgrtd', probs, v)
        out = out.reshape(B, H, T, D).transpose(0, 2, 1, 3).reshape(B, T, H * D)
        return out @ Wo + bo

    def _L0_ffn_ref(hidden_states, Wq, Wr, aux_keys, aux_values, Wvd, Wvu, Wu1, bu1, Wu2, bu2, gate_w1, gate_bias, log_rel):
        import jax, jax.numpy as jnp
        import numpy as np
        HID, BOT, RDIM, NSLOT, K, VB = (512, 64, 48, 128, 8, 32)
        TAU_LOW, TAU_HIGH, EARLY_EXIT = (0.5, 2.0, 0.05)

        def _uncertainty(h, Wu1, bu1, Wu2, bu2):
            var = jnp.var(h, axis=-1)
            log_var = jnp.log1p(var)
            norm_var = log_var / (jnp.mean(log_var) + 1e-06)
            learned = (jax.nn.gelu(h @ Wu1.T + bu1) @ Wu2.T + bu2)[..., 0]
            return jnp.clip(norm_var * 0.5 + jax.nn.sigmoid(learned) * 2.5, 0.0, 5.0)
        query = hidden_states @ Wq.T
        rq = query @ Wr.T
        rk = aux_keys @ Wr.T
        router_scores = jnp.einsum('bsr,nr->bsn', rq, rk) / np.sqrt(RDIM) + log_rel
        top_scores, top_idx = jax.lax.top_k(router_scores, K)
        sel_keys = aux_keys[top_idx]
        attn = jnp.einsum('bsd,bskd->bsk', query, sel_keys) / np.sqrt(BOT) + log_rel[top_idx]
        w = jax.nn.softmax(attn, axis=-1)
        sel_vals = aux_values[top_idx]
        aux_out = jnp.einsum('bsk,bskh->bsh', w, sel_vals)
        aux_out = aux_out @ Wvd.T @ Wvu.T
        u = _uncertainty(hidden_states, Wu1, bu1, Wu2, bu2)
        u_norm = jnp.clip((u - TAU_LOW) / (TAU_HIGH - TAU_LOW), 0.0, 1.0)
        gate = jax.nn.sigmoid(gate_w1 * u_norm + gate_bias)
        gate = jnp.where(gate < EARLY_EXIT, 0.0, gate)
        return hidden_states + gate[..., None] * aux_out
    x = L0_attn_x
    x = x + 0.5 * _L0_ffn_ref(_layernorm(x, axis=-1), L0_ffn_Wq, L0_ffn_Wr, L0_ffn_aux_keys, L0_ffn_aux_values, L0_ffn_Wvd, L0_ffn_Wvu, L0_ffn_Wu1, L0_ffn_bu1, L0_ffn_Wu2, L0_ffn_bu2, L0_ffn_gate_w1, L0_ffn_gate_bias, L0_ffn_log_rel)
    x = x + _L0_attn_ref(_layernorm(x, axis=-1), L0_attn_Wq, L0_attn_Wk, L0_attn_Wv, L0_attn_Wo, L0_attn_bo)
    x = x + 0.5 * _L0_ffn_ref(_layernorm(x, axis=-1), L0_ffn_Wq, L0_ffn_Wr, L0_ffn_aux_keys, L0_ffn_aux_values, L0_ffn_Wvd, L0_ffn_Wvu, L0_ffn_Wu1, L0_ffn_bu1, L0_ffn_Wu2, L0_ffn_bu2, L0_ffn_gate_w1, L0_ffn_gate_bias, L0_ffn_log_rel)
    return x

_drawn_inputs = setup_inputs


def setup_inputs(seed=0):
    import zlib

    import numpy as np

    out = dict(_drawn_inputs(seed))
    spreads = {'L0_attn_bo': (0.0, 0.1), 'L0_ffn_bu1': (0.0, 2.0), 'L0_ffn_log_rel': (0.0, 2.0)}
    factors = {'L0_ffn_Wq': 48.242,
     'L0_ffn_Wr': 58.716,
     'L0_ffn_aux_keys': 48.189,
     'L0_ffn_aux_values': 47.029,
     'L0_ffn_Wvd': 46.835,
     'L0_ffn_Wvu': 46.345,
     'L0_ffn_Wu1': 64.0,
     'L0_ffn_Wu2': 64.0}
    for name, (base, spread) in spreads.items():
        noise = np.random.default_rng([zlib.crc32(name.encode()), seed]).standard_normal(out[name].shape)
        drawn = base * np.exp(spread * noise) if base else spread * noise
        out[name] = jnp.asarray(drawn.astype(out[name].dtype))
    for name, factor in factors.items():
        out[name] = (out[name] * factor).astype(out[name].dtype)
    return out
```

```python
from contextlib import ExitStack

import concourse.bass as bass
from concourse import mybir

ALU = mybir.AluOpType
ACT = mybir.ActivationFunctionType
F32 = mybir.dt.float32
BF16 = mybir.dt.bfloat16
F16 = mybir.dt.float16
AX_X = mybir.AxisListType.X

P = 128
B, T, C = 4, 512, 512
NT = B * T // P
TB = T // P
CC = C // P
G, HG, D = 8, 4, 128
SCALE = float(D) ** -0.5
BOT, RDIM, NSLOT, VB = 64, 48, 128, 32
EPS = 1e-5
TAU_LOW, TAU_HIGH, EARLY_EXIT = 0.5, 2.0, 0.05
PSCALE = 1024.0
MASKED = 1e30
SELECTED = -3e38
SOFF = [896, 1024, 512, 0]
SBANKS = [[3], [2, 0], [1]]
TOFF = [0, 512, 896, 1152]
NP_ = 1280
PIECES = ["K", "Q0", "Q1", "V", "Q2", "Q3"]
NPC = len(PIECES)


def macaron_kernel(nc: bass.Bass, x, wqkv, wo, bo, cosq, sinq, cosk, sink,
                   f_wq, f_wr, f_wrT, f_keyT, f_valT, f_wvdT, f_wvuT, f_wu1T, f_bu1, f_wu2T,
                   f_bu2, f_gw, f_gb, f_lr, out):
    ctx = ExitStack()
    with ctx:
        def sb(name, shape, dt):
            return ctx.enter_context(nc.sbuf_tensor(name, shape, dt))

        def pb(name, shape, dt):
            return ctx.enter_context(nc.psum_tensor(name, shape, dt))

        def sem(name):
            return ctx.enter_context(nc.semaphore(name))

        X = sb("X", [P, NT, C], F32)
        XTh = sb("XTh", [P, CC, B * T], F16)
        XTl = sb("XTl", [P, CC, B * T], F16)
        cq, sq = sb("cq", [P, T], F32), sb("sq", [P, T], F32)
        ck, sk = sb("ck", [P, T], F32), sb("sk", [P, T], F32)
        wraw = sb("wraw", [P, NPC, CC, D], F32)
        wh = sb("wh", [P, NPC, CC, D], BF16)
        wl = sb("wl", [P, NPC, CC, D], F16)
        woraw = sb("woraw", [P, HG, C], F32)
        woh = sb("woh", [P, HG, C], BF16)
        wol = sb("wol", [P, HG, C], F16)
        kTh, kTl = sb("kTh", [P, 2, T], BF16), sb("kTl", [P, 2, T], F16)
        vh, vl = sb("vh", [P, 2, TB, D], BF16), sb("vl", [P, 2, TB, D], F16)
        qTh, qTl = sb("qTh", [P, HG, T], BF16), sb("qTl", [P, HG, T], F16)
        t1, t2 = sb("t1", [P, 2, T], F32), sb("t2", [P, 2, T], F32)
        p = sb("p", [P, 2, NP_], F32)
        pTh, pTl = sb("pTh", [P, NP_], F16), sb("pTl", [P, NP_], F16)
        oTh, oTl = sb("oTh", [P, 2, HG, T], BF16), sb("oTl", [P, 2, HG, T], F16)
        mn, rs, ri = sb("mn", [P, 2, TB], F32), sb("rs", [P, 2, TB], F32), sb("ri", [P, 2, TB], F32)
        ident = sb("ident", [P, P], F32)
        identb = sb("identb", [P, P], BF16)
        maskb = sb("maskb", [P, P], BF16)
        ones = sb("ones", [P, P], F32)
        bob = sb("bob", [P, C], F32)
        st = sb("st", [P, NT, 6], F32)
        mv = sb("mv", [P, NT, 2], F32)
        ve, sd, rstd, nw = (sb(n, [P, NT], F32) for n in ("ve", "sd", "rstd", "nw"))
        hbuf = sb("hbuf", [P, 2, C], F32)
        fwq = sb("fwq", [BOT, C], F32)
        fwr, fwrT = sb("fwr", [RDIM, BOT], F32), sb("fwrT", [BOT, RDIM], F32)
        fkeyT = sb("fkeyT", [BOT, NSLOT], F32)
        fvalT, fwvdT = sb("fvalT", [P, CC, NSLOT], F32), sb("fwvdT", [P, CC, VB], F32)
        fwvuT = sb("fwvuT", [VB, C], F32)
        fwu1T = sb("fwu1T", [P, CC, P], F32)
        bu1, wu2T = sb("bu1", [P, 1], F32), sb("wu2T", [P, 1], F32)
        bu2, gw, gb = sb("bu2", [P, 1], F32), sb("gw", [P, 1], F32), sb("gb", [P, 1], F32)
        lrb = sb("lrb", [P, NSLOT], F32)
        rk = sb("rk", [RDIM, NSLOT], F32)
        rmat = sb("rmat", [BOT, NSLOT], F32)
        u1T = sb("u1T", [VB, NSLOT], F32)
        ah, al = sb("ah", [P, CC, 2 * NSLOT], BF16), sb("al", [P, CC, 2 * NSLOT], F16)
        v2h, v2l = sb("v2h", [P, C], BF16), sb("v2l", [P, C], F16)
        uh, ul = sb("uh", [P, CC, P], BF16), sb("ul", [P, CC, P], F16)
        gT = t2
        lv, lsum = sb("lv", [P, NT], F32), sb("lsum", [P, 1], F32)
        gt, gt2, gt3, gate = (sb(n, [P, NT], F32) for n in ("gt", "gt2", "gt3", "gate"))
        rsc = p[:, 0, 0:T].rearrange("p (t n) -> p t n", t=TB)
        asc = p[:, 0, T:2 * T].rearrange("p (t n) -> p t n", t=TB)
        mr = t1[:, 0, :].rearrange("p (t n) -> p t n", t=TB)
        ee = p[:, 1, 0:2 * T].rearrange("p (c t n) -> p c t n", c=2, t=TB)
        m8 = sb("m8", [P, TB, 8], F32)
        mx, sm, gs = sb("mx", [P, TB], F32), sb("sm", [P, TB], F32), sb("gs", [P, 2, TB], F32)
        eTh, eTl = sb("eTh", [P, T], F16), sb("eTl", [P, T], F16)

        PJ = pb("PJ", [P, 2, T], F32)
        SC = pb("SC", [P, 3, T], F32)
        TR = pb("TR", [P, 2, T], F32)
        PV = pb("PV", [P, T], F32)
        SCf = SC[:, :, :].rearrange("p b n -> p (b n)")

        ld_x = [sem(f"ld_x{i}") for i in range(4)]
        ld_f = sem("ld_f")
        ld_w = sem("ld_w")
        ld_wo = sem("ld_wo")
        st_out = sem("st_out")
        cst0, cst = sem("cst0"), sem("cst")
        dch = sem("dch")
        fs_pe, fs_ev = sem("fs_pe"), sem("fs_ev")
        fs_hi, fs_lo = sem("fs_hi"), sem("fs_lo")
        ln_v, ln_sd = sem("ln_v"), sem("ln_sd")
        ln_h, ln_t = sem("ln_h"), sem("ln_t")
        ln_hi, ln_lo = sem("ln_hi"), sem("ln_lo")
        bo_add = sem("bo_add")
        u_ps, u_g, u_l = sem("u_ps"), sem("u_g"), sem("u_l")
        g_lv, g_sum, g_ps = sem("g_lv"), sem("g_sum"), sem("g_ps")
        g_ex, g_exd = sem("g_ex"), sem("g_exd")
        r_sc, r_use = sem("r_sc"), sem("r_use")
        r_am, r_e = sem("r_am"), sem("r_e")
        r_t, r_hi, r_lo = sem("r_t"), sem("r_hi"), sem("r_lo")
        r_aux, r_x = sem("r_aux"), sem("r_x")
        w_hi, w_lo = sem("w_hi"), sem("w_lo")
        wo_hi, wo_lo = sem("wo_hi"), sem("wo_lo")
        s_q, s_k, s_v, s_o = sem("s_q"), sem("s_k"), sem("s_v"), sem("s_o")
        rope_mul, rope_sum = sem("rope_mul"), sem("rope_sum")
        rope_hi, rope_lo = sem("rope_hi"), sem("rope_lo")
        v_hi, v_lo = sem("v_hi"), sem("v_lo")
        s_sc, d_min, a_exp = sem("s_sc"), sem("d_min"), sem("a_exp")
        d_norm = sem("d_norm")
        s_tr, tr_hi, tr_lo = sem("s_tr"), sem("tr_hi"), sem("tr_lo")
        s_pv, o_hi, o_lo = sem("s_pv"), sem("o_hi"), sem("o_lo")
        o_add = sem("o_add")

        x_v = x.rearrange("(n p) c -> p n c", p=P)
        out_v = out.rearrange("(n p) c -> p n c", p=P)

        def tasks_of(n, h):
            q = [("Q", n, h + 2, 0)] if h < 2 else [("Q", n + 1, h - 2, 3 - h)]
            rest = {0: [("K", n + 1, 0, 1)],
                    1: [("O", n - 1, 0, 1), ("O", n - 1, 1, 0)],
                    2: [("V", n + 1, 0, 0), ("O", n - 1, 2, 1)],
                    3: [("O", n - 1, 3, 1)]}[h]
            ok = lambda t: 0 <= t[1] < G * B
            return [t for t in q if ok(t)], [t for t in rest if ok(t)]

        PROLOGUE = [("K", 0, 0, 0), ("V", 0, 0, 1), ("Q", 0, 0, 1), ("Q", 0, 1, 0)]
        EPILOGUE = [("O", G * B - 1, i, (i + 1) % 2) for i in range(TB)]
        ALL = list(PROLOGUE)
        for n_ in range(G * B):
            for h_ in range(HG):
                a_, b_ = tasks_of(n_, h_)
                ALL += a_ + b_
        ALL += EPILOGUE
        BEFORE, last_of = {}, {}
        for t_ in ALL:
            BEFORE[t_[:3]] = last_of.get(t_[3])
            last_of[t_[3]] = t_

        def rope_index(kind, n, idx, n0):
            if kind == "K":
                return 0 if n0 == 0 else 5 * n - 1
            return 5 * n + (1, 2, 3, 5 if n0 < G * B - 1 else 4)[idx]

        def consumed(kind, n, idx, n0):
            if kind in "QK":
                return rope_mul, rope_index(kind, n, idx, n0) + 1
            if kind == "V":
                return v_lo, n + 1
            return o_add, 4 * n + idx + 1

        def rep(g, first, last):
            return 0 if first else (G - 1 if last else 3)

        def bodies(eng, body):
            body(0, True, False)
            with eng.Fori(1, G - 1) as g:
                body(g, False, False)
            body(G - 1, False, True)

        block = ctx.enter_context(nc.Block())

        @block.sync
        def _(sp):
            for i in range(4):
                sp.dma_start(X[:, 4 * i:4 * i + 4, :], x_v[:, 4 * i:4 * i + 4, :]).then_inc(ld_x[i], 16)
            fl = [(fwq[:, :], f_wq), (fwr[:, :], f_wr), (fwrT[:, :], f_wrT), (fkeyT[:, :], f_keyT),
                  (fvalT[:, :, :], f_valT.rearrange("(c p) n -> p c n", p=P)),
                  (fwvdT[:, :, :], f_wvdT.rearrange("(c p) n -> p c n", p=P)),
                  (fwvuT[:, :], f_wvuT), (fwu1T[:, :, :], f_wu1T.rearrange("(c p) n -> p c n", p=P)),
                  (bu1[:, :], f_bu1), (wu2T[:, :], f_wu2T),
                  (bu2[:, :], f_bu2.to_broadcast([P, 1])), (gw[:, :], f_gw.to_broadcast([P, 1])),
                  (gb[:, :], f_gb.to_broadcast([P, 1])), (lrb[:, :], f_lr.to_broadcast([P, NSLOT])),
                  (bob[:, :], bo.to_broadcast([P, C])),
                  (cq[:, :], cosq), (sq[:, :], sinq), (ck[:, :], cosk), (sk[:, :], sink)]
            assert len(fl) == NFL
            for dst, src in fl:
                sp.dma_start(dst, src).then_inc(ld_f, 16)
            sp.dma_start(wraw[:, :, :, :], wqkv[0]).then_inc(ld_w, 16)
            sp.dma_start(woraw[:, :, :], wo[0]).then_inc(ld_wo, 16)

            def body(g, first, last):
                if not last:
                    sp.wait_ge(w_lo, NPC * g + NPC)
                    sp.dma_start(wraw[:, :, :, :], wqkv[g + 1]).then_inc(ld_w, 16)
                    sp.wait_ge(wo_lo, HG * g + HG)
                    sp.dma_start(woraw[:, :, :], wo[g + 1]).then_inc(ld_wo, 16)
            bodies(sp, body)
            for i in range(4):
                sp.wait_ge(r_x, NT + 4 * i + 4)
                sp.dma_start(out_v[:, 4 * i:4 * i + 4, :], X[:, 4 * i:4 * i + 4, :]).then_inc(st_out, 16)
            sp.wait_ge(st_out, 64)

        @block.gpsimd
        def _(pool):
            nc.gpsimd.memset(ident[:, :], 0.0)
            nc.gpsimd.memset(identb[:, :], 0.0)
            nc.gpsimd.memset(maskb[:, :], 0.0)
            nc.gpsimd.memset(ones[:, :], 1.0).then_inc(cst0, 1)
            pool.wait_ge(cst0, 1)
            for m in (ident, identb):
                nc.gpsimd.affine_select(out=m[:, :], in_=m[:, :], compare_op=ALU.not_equal, fill=1.0,
                                        base=0, pattern=[[-1, P]], channel_multiplier=1)
            nc.gpsimd.affine_select(out=maskb[:, :], in_=maskb[:, :], compare_op=ALU.is_ge, fill=MASKED,
                                    base=0, pattern=[[-1, P]], channel_multiplier=1).then_inc(cst, 1)

            pool.wait_ge(ld_f, 16 * NFL)
            for n in range(NT):
                pool.wait_ge(ln_h, NT + n + 1)
                nc.gpsimd.tensor_tensor(X[:, n, :], X[:, n, :], bob[:, :], ALU.add).then_inc(bo_add, 1)

            def w_low(g, k):
                pool.wait_ge(w_hi, NPC * g + k + 1)
                nc.gpsimd.tensor_tensor(wl[:, k, :, :], wraw[:, k, :, :], wh[:, k, :, :],
                                        ALU.subtract).then_inc(w_lo, 1)

            def rope(kind, n, idx, n0, par):
                r = rope_index(kind, n, idx, n0)
                j = rope_index(kind, n0, idx, n0) % 2
                pool.wait_ge(rope_mul, r + 1)
                nc.gpsimd.tensor_tensor(t1[:, j, :], t1[:, j, :], t2[:, j, :], ALU.add).then_inc(rope_sum, 1)
                pool.wait_ge(rope_hi, r + 1)
                hi, lo = (qTh[:, idx, :], qTl[:, idx, :]) if kind == "Q" else (kTh[:, par, :], kTl[:, par, :])
                nc.gpsimd.tensor_tensor(lo, t1[:, j, :], hi, ALU.subtract).then_inc(rope_lo, 1)

            for k in range(NPC):
                w_low(0, k)
            for kind, n, idx, _ in PROLOGUE:
                if kind in "QK":
                    rope(kind, n, idx, n, n % 2)

            def body(g, first, last):
                g0 = rep(g, first, last)
                for b in range(B):
                    for h in range(HG):
                        n, n0 = B * g + b, B * g0 + b
                        if b == 1 and h == 0:
                            for k in range(HG):
                                pool.wait_ge(wo_hi, HG * g + k + 1)
                                nc.gpsimd.tensor_tensor(wol[:, k, :], woraw[:, k, :], woh[:, k, :],
                                                        ALU.subtract).then_inc(wo_lo, 1)
                        qs, rest = tasks_of(n0, h)
                        for kind, m0, idx, _ in qs + rest:
                            if kind in "QK":
                                rope(kind, n + (m0 - n0), idx, m0, m0 % 2)
                        if not last:
                            for k in SPLIT_AT.get((b, h), []):
                                w_low(g + 1, k)
            bodies(pool, body)

        @block.scalar
        def _(act):
            act.wait_ge(ld_f, 16 * NFL)
            nc.scalar.copy(uh[:, :, :], fwu1T[:, :, :]).then_inc(fs_hi, 1)
            for c in range(CC):
                act.wait_ge(fs_pe, 5 + c)
                nc.scalar.copy(ah[:, c, :], PJ[:, c % 2, 0:2 * NSLOT]).then_inc(fs_hi, 1)
            act.wait_ge(fs_pe, 9)
            nc.scalar.copy(v2h[:, :], PV[:, :]).then_inc(fs_hi, 1)

            def layernorm(k):
                act.wait_ge(ln_v, k + 1)
                nc.scalar.activation(sd[:, :], ve[:, :], ACT.Sqrt).then_inc(ln_sd, 1)
                with act.Fori(0, NT // 2) as m:
                    for i in range(2):
                        act.wait_ge(ln_t, NT * k + 2 * m + i + 1)
                        nc.scalar.copy(XTh[:, :, bass.ds(m * 2 * P + i * P, P)],
                                       TR[:, i, :].rearrange("p (c t) -> p c t", c=CC)).then_inc(ln_hi, 1)

            def ffn(f):
                for c in range(4):
                    act.wait_ge(u_ps, 4 * f + c + 1)
                    if 4 * f + c >= 2:
                        act.wait_ge(u_l, 4 * f + c - 1)
                    nc.scalar.activation(gT[:, c % 2, :], PJ[:, c % 2, :], ACT.Gelu_apprx_tanh,
                                         bias=bu1[:, 0:1]).then_inc(u_g, 1)
                act.wait_ge(g_lv, 2 * f + 1)
                nc.scalar.activation(lv[:, :], gt[:, :], ACT.Ln, bias=1.0).then_inc(g_lv, 1)
                for k in range(2):
                    act.wait_ge(g_ex, 2 * f + k + 1)
                    nc.scalar.activation(gt2[:, :], gt[:, :], ACT.Exp, scale=-1.0).then_inc(g_exd, 1)
                for c in range(4):
                    act.wait_ge(r_am, 4 * f + c + 1)
                    nc.scalar.activation(ee[:, c % 2, :, :], ee[:, c % 2, :, :], ACT.Exp).then_inc(r_e, 1)
                    act.wait_ge(r_t, 4 * f + c + 1)
                    nc.scalar.copy(eTh[:, :], TR[:, 0, :]).then_inc(r_hi, 1)

            layernorm(0)
            ffn(0)
            layernorm(1)

            def w_high(g, k, wait):
                act.wait_ge(ld_w, 16 * g + 16)
                if wait:
                    act.wait_ge(*wait)
                nc.scalar.copy(wh[:, k, :, :], wraw[:, k, :, :]).then_inc(w_hi, 1)

            def rope(kind, n, idx, n0, par):
                r = rope_index(kind, n, idx, n0)
                j = rope_index(kind, n0, idx, n0) % 2
                act.wait_ge(rope_sum, r + 1)
                hi = qTh[:, idx, :] if kind == "Q" else kTh[:, par, :]
                nc.scalar.copy(hi, t1[:, j, :]).then_inc(rope_hi, 1)

            def value_hi(n, n0, bank):
                act.wait_ge(s_v, n + 1)
                nc.scalar.copy(vh[:, n0 % 2, :, :],
                               PJ[:, bank, :].rearrange("p (a d) -> p a d", a=TB)).then_inc(v_hi, 1)

            def p_hi(s, j):
                act.wait_ge(s_tr, 4 * s + j + 1)
                w = (TB - j) * P
                nc.scalar.copy(pTh[:, TOFF[j]:TOFF[j] + w], TR[:, j % 2, 0:w]).then_inc(tr_hi, 1)

            def out_hi(s, b, h):
                act.wait_ge(s_pv, s + 1)
                nc.scalar.mul(oTh[:, b % 2, h, :], PV[:, :], 1.0 / PSCALE).then_inc(o_hi, 1)

            for k in range(NPC):
                w_high(0, k, None)
            for kind, n, idx, bank in PROLOGUE:
                if kind in "QK":
                    rope(kind, n, idx, n, n % 2)
                if kind == "V":
                    value_hi(n, n, bank)

            def body(g, first, last):
                g0 = rep(g, first, last)
                for b in range(B):
                    for h in range(HG):
                        n, n0 = B * g + b, B * g0 + b
                        s = 4 * n + h
                        prev = not (first and b == 0 and h == 0)
                        pb_, ph_ = ((b - 1) % B if h == 0 else b), (h - 1) % HG
                        if prev:
                            p_hi(s - 1, 0)
                            p_hi(s - 1, 1)
                        for k, tiles in enumerate(SBANKS):
                            act.wait_ge(d_min, 3 * s + k + 1)
                            for i in tiles:
                                w = (i + 1) * P
                                ins = nc.scalar.activation(
                                    p[:, h % 2, SOFF[i]:SOFF[i] + w], SCf[:, SOFF[i]:SOFF[i] + w], ACT.Exp,
                                    bias=mn[:, h % 2, i:i + 1], scale=-1.0, accum_out=rs[:, h % 2, i:i + 1])
                            ins.then_inc(a_exp, 1)
                        if prev:
                            p_hi(s - 1, 2)
                            p_hi(s - 1, 3)
                        if b == 1 and h == 0:
                            act.wait_ge(ld_wo, 16 * g + 16)
                            if not first:
                                act.wait_ge(s_o, 16 * g)
                            for k in range(HG):
                                nc.scalar.copy(woh[:, k, :], woraw[:, k, :]).then_inc(wo_hi, 1)
                        qs, rest = tasks_of(n0, h)
                        for kind, m0, idx, _ in qs:
                            rope(kind, n + (m0 - n0), idx, m0, m0 % 2)
                        if prev:
                            out_hi(s - 1, pb_, ph_)
                        for kind, m0, idx, bank in rest:
                            if kind == "K":
                                rope(kind, n + (m0 - n0), idx, m0, m0 % 2)
                            if kind == "V":
                                value_hi(n + (m0 - n0), m0, bank)
                        if not last:
                            for k in SPLIT_AT.get((b, h), []):
                                pc = PIECES[k]
                                reader = {"K": (s_k, 4 * g + 4), "V": (s_v, 4 * g + 4)}.get(
                                    pc, (s_q, 16 * g + 12 + int(pc[1:] or 0) + 1 if pc[0] == "Q" else 0))
                                w_high(g + 1, k, reader)
            bodies(act, body)
            SL = G * B * HG
            for j in range(TB):
                p_hi(SL - 1, j)
            out_hi(SL - 1, B - 1, HG - 1)

            layernorm(2)
            ffn(1)

        @block.vector
        def _(dve):
            chain = [0]

            def link(ins):
                chain[0] += 1
                ins.then_inc(dch, 1)
                dve.wait_ge(dch, chain[0])

            dve.wait_ge(fs_pe, 1)
            nc.vector.tensor_copy(rk[:, :], PV[0:RDIM, 0:NSLOT]).then_inc(fs_ev, 1)
            dve.wait_ge(fs_pe, 2)
            nc.vector.tensor_copy(rmat[:, :], TR[0:BOT, 0, 0:NSLOT]).then_inc(fs_ev, 1)
            dve.wait_ge(fs_pe, 4)
            nc.vector.tensor_copy(u1T[:, :], SC[0:VB, 0, 0:NSLOT]).then_inc(fs_ev, 1)
            dve.wait_ge(fs_hi, 1)
            nc.vector.tensor_tensor(ul[:, :, :], fwu1T[:, :, :], uh[:, :, :], ALU.subtract).then_inc(fs_lo, 1)
            for c in range(CC):
                dve.wait_ge(fs_hi, c + 2)
                nc.vector.tensor_tensor(al[:, c, :], PJ[:, c % 2, 0:2 * NSLOT], ah[:, c, :],
                                        ALU.subtract).then_inc(fs_lo, 1)
            dve.wait_ge(fs_hi, 6)
            nc.vector.tensor_tensor(v2l[:, :], PV[:, :], v2h[:, :], ALU.subtract).then_inc(fs_lo, 1)

            def layernorm(k, half):
                for n in range(NT):
                    if k == 0 and n % 4 == 0:
                        dve.wait_ge(ld_x[n // 4], 16)
                    ins = nc.vector.bn_stats(st[:, n, :], X[:, n, :])
                link(ins)
                for n in range(NT):
                    ins = nc.vector.bn_aggr(mv[:, n, :], st[:, n, :])
                link(ins)
                nc.vector.tensor_scalar_add(ve[:, :], mv[:, :, 1], EPS).then_inc(ln_v, 1)
                dve.wait_ge(ln_sd, k + 1)
                link(nc.vector.reciprocal(rstd[:, :], sd[:, :]))
                link(nc.vector.tensor_tensor(nw[:, :], rstd[:, :], rstd[:, :], ALU.mult))
                link(nc.vector.tensor_tensor(nw[:, :], nw[:, :], ve[:, :], ALU.mult))
                link(nc.vector.tensor_scalar(nw[:, :], nw[:, :], -0.5, 1.5, ALU.mult, ALU.add))
                link(nc.vector.tensor_tensor(rstd[:, :], rstd[:, :], nw[:, :], ALU.mult))

                def normal(n, i):
                    return nc.vector.tensor_scalar(hbuf[:, i, :], X[:, bass.ds(n, 1), :].rearrange("p a c -> p (a c)"),
                                                   mv[:, bass.ds(n, 1), 0], rstd[:, bass.ds(n, 1)],
                                                   ALU.subtract, ALU.mult)
                with dve.Fori(0, NT // 2) as m:
                    for i in range(2):
                        n = m * 2 + i
                        if k == 0:
                            pass
                        normal(n, i).then_inc(ln_h, 1)
                        if half:
                            dve.wait_ge(ln_h, NT * k + 2 * m + i + 1)
                            xt = X[:, bass.ds(n, 1), :].rearrange("p a c -> p (a c)")
                            nc.vector.scalar_tensor_tensor(out=xt, in0=hbuf[:, i, :], scalar=0.5, in1=xt,
                                                           op0=ALU.mult, op1=ALU.add)
                        dve.wait_ge(ln_hi, NT * k + 2 * m + i + 1)
                        cols = bass.ds(m * 2 * P + i * P, P)
                        nc.vector.tensor_tensor(XTl[:, :, cols], TR[:, i, :].rearrange("p (c t) -> p c t", c=CC),
                                                XTh[:, :, cols], ALU.subtract).then_inc(ln_lo, 1)

            def ffn(f):
                link(nc.vector.reciprocal(gt2[:, :], ve[:, :]))
                nc.vector.tensor_tensor(gt[:, :], mv[:, :, 1], gt2[:, :], ALU.mult).then_inc(g_lv, 1)
                dve.wait_ge(g_lv, 2 * f + 2)
                nc.vector.reduce_sum(lsum[:, :], lv[:, :], AX_X).then_inc(g_sum, 1)
                dve.wait_ge(g_ps, f + 1)
                link(nc.vector.tensor_scalar(lsum[:, :], PV[:, NT:NT + 1], 1.0 / (B * T), 1e-6, ALU.mult, ALU.add))
                link(nc.vector.reciprocal(lsum[:, :], lsum[:, :]))
                link(nc.vector.tensor_scalar(gt3[:, :], lv[:, :], lsum[:, 0:1], 0.5, ALU.mult, ALU.mult))

                def sigmoid_from(k):
                    nc.vector.tensor_scalar_max(gt[:, :], gt[:, :], -80.0).then_inc(g_ex, 1)
                    dve.wait_ge(g_exd, 2 * f + k + 1)
                    link(nc.vector.tensor_scalar_add(gt2[:, :], gt2[:, :], 1.0))
                    link(nc.vector.reciprocal(gt2[:, :], gt2[:, :]))

                link(nc.vector.tensor_scalar(gt[:, :], PV[:, 0:NT], bu2[:, 0:1], None, ALU.add))
                sigmoid_from(0)
                link(nc.vector.scalar_tensor_tensor(out=gt3[:, :], in0=gt2[:, :], scalar=2.5, in1=gt3[:, :],
                                                    op0=ALU.mult, op1=ALU.add))
                link(nc.vector.tensor_scalar(gt3[:, :], gt3[:, :], 0.0, 5.0, ALU.max, ALU.min))
                link(nc.vector.tensor_scalar(gt3[:, :], gt3[:, :], -TAU_LOW, 1.0 / (TAU_HIGH - TAU_LOW),
                                             ALU.add, ALU.mult))
                link(nc.vector.tensor_scalar(gt3[:, :], gt3[:, :], 0.0, 1.0, ALU.max, ALU.min))
                link(nc.vector.tensor_scalar(gt[:, :], gt3[:, :], gw[:, 0:1], gb[:, 0:1], ALU.mult, ALU.add))
                sigmoid_from(1)
                link(nc.vector.tensor_scalar(gt3[:, :], gt2[:, :], EARLY_EXIT, 0.5, ALU.is_ge, ALU.mult))
                link(nc.vector.tensor_tensor(gate[:, :], gt2[:, :], gt3[:, :], ALU.mult))

                def select_slots(c):
                    e = ee[:, c % 2, :, :]
                    for k in range(2):
                        bank = (SC if c % 2 == 0 else PJ)[:, k, :].rearrange("p (t n) -> p t n", t=2)
                        lr2 = lrb[:, :].unsqueeze(1).to_broadcast([P, 2, NSLOT])
                        dve.wait_ge(r_sc, 8 * f + 2 * c + k + 1)
                        nc.vector.scalar_tensor_tensor(out=rsc[:, 2 * k:2 * k + 2, :], in0=bank[:, :, 0:NSLOT],
                                                       scalar=RDIM ** -0.5, in1=lr2, op0=ALU.mult, op1=ALU.add)
                        ins = nc.vector.scalar_tensor_tensor(out=asc[:, 2 * k:2 * k + 2, :],
                                                             in0=bank[:, :, NSLOT:2 * NSLOT],
                                                             scalar=BOT ** -0.5, in1=lr2, op0=ALU.mult, op1=ALU.add)
                        ins.then_inc(r_use, 1)
                    dve.wait_ge(r_use, 8 * f + 2 * c + 2)
                    for i in range(TB):
                        ins = nc.vector.max(m8[:, i, :], rsc[:, i, :])
                    link(ins)
                    for i in range(TB):
                        ins = nc.vector.match_replace(mr[:, i, :], m8[:, i, :], rsc[:, i, :], SELECTED)
                    link(ins)
                    link(nc.vector.tensor_scalar(mr[:, :, :], mr[:, :, :], 0.99 * SELECTED, -MASKED,
                                                 ALU.is_gt, ALU.mult))
                    link(nc.vector.tensor_tensor(asc[:, :, :], asc[:, :, :], mr[:, :, :], ALU.add))
                    link(nc.vector.reduce_max(mx[:, :], asc[:, :, :], AX_X))
                    nc.vector.tensor_tensor(e, asc[:, :, :], mx[:, :].unsqueeze(2).to_broadcast([P, TB, NSLOT]),
                                            ALU.subtract).then_inc(r_am, 1)
                    dve.wait_ge(r_e, 4 * f + c + 1)
                    link(nc.vector.reduce_sum(sm[:, :], e, AX_X))
                    link(nc.vector.reciprocal(sm[:, :], sm[:, :]))
                    link(nc.vector.tensor_tensor(gs[:, c % 2, :], sm[:, :], gate[:, 4 * c:4 * c + 4], ALU.mult))

                def finish(c):
                    dve.wait_ge(r_hi, 4 * f + c + 1)
                    nc.vector.tensor_tensor(eTl[:, :], TR[:, 0, :], eTh[:, :], ALU.subtract).then_inc(r_lo, 1)
                    for i in range(TB):
                        n = 4 * c + i
                        dve.wait_ge(r_aux, NT * f + n + 1)
                        bank = SC[:, 2, :] if i % 2 == 0 else PV[:, :]
                        nc.vector.scalar_tensor_tensor(out=X[:, n, :], in0=bank, scalar=gs[:, c % 2, i:i + 1],
                                                       in1=X[:, n, :], op0=ALU.mult, op1=ALU.add).then_inc(r_x, 1)
                select_slots(0)
                for c in range(1, 4):
                    select_slots(c)
                    finish(c - 1)
                finish(3)
                dve.wait_ge(r_x, NT * f + NT)

            layernorm(0, True)
            ffn(0)
            layernorm(1, False)

            dve.wait_ge(bo_add, NT)
            dve.wait_ge(ld_f, 16 * NFL)

            def rope(kind, n, idx, n0, bank):
                r = rope_index(kind, n, idx, n0)
                r0 = rope_index(kind, n0, idx, n0)
                j, (c_, s_) = r0 % 2, ((cq, sq) if kind == "Q" else (ck, sk))
                if kind == "Q":
                    dve.wait_ge(s_q, 4 * n + idx + 1)
                else:
                    dve.wait_ge(s_k, n + 1)
                if r0 >= 2:
                    dve.wait_ge(rope_lo, r - 1)
                H = P // 2
                nc.vector.tensor_tensor(t1[:, j, :], PJ[:, bank, :], c_[:, :], ALU.mult)
                nc.vector.tensor_tensor(t2[0:H, j, :], PJ[H:P, bank, :], s_[0:H, :], ALU.mult)
                nc.vector.tensor_tensor(t2[H:P, j, :], PJ[0:H, bank, :], s_[H:P, :], ALU.mult).then_inc(rope_mul, 1)

            def value_lo(n, n0, bank):
                dve.wait_ge(v_hi, n + 1)
                nc.vector.tensor_tensor(vl[:, n0 % 2, :, :], PJ[:, bank, :].rearrange("p (a d) -> p a d", a=TB),
                                        vh[:, n0 % 2, :, :], ALU.subtract).then_inc(v_lo, 1)

            def project_add(n, i, b, bank):
                dve.wait_ge(s_o, 4 * n + i + 1)
                xt = X[:, TB * b + i, :]
                nc.vector.tensor_tensor(xt, PJ[:, bank, :], xt, ALU.add).then_inc(o_add, 1)

            def p_lo(s, j):
                dve.wait_ge(tr_hi, 4 * s + j + 1)
                w = (TB - j) * P
                nc.vector.tensor_tensor(pTl[:, TOFF[j]:TOFF[j] + w], TR[:, j % 2, 0:w], pTh[:, TOFF[j]:TOFF[j] + w],
                                        ALU.subtract).then_inc(tr_lo, 1)

            def out_lo(s, b, h):
                dve.wait_ge(o_hi, s + 1)
                nc.vector.scalar_tensor_tensor(out=oTl[:, b % 2, h, :], in0=PV[:, :], scalar=1.0 / PSCALE,
                                               in1=oTh[:, b % 2, h, :], op0=ALU.mult,
                                               op1=ALU.subtract).then_inc(o_lo, 1)

            for kind, n, idx, bank in PROLOGUE:
                if kind in "QK":
                    rope(kind, n, idx, n, bank)
                if kind == "V":
                    value_lo(n, n, bank)

            d_rec = sem("d_rec")

            def body(g, first, last):
                g0 = rep(g, first, last)
                for b in range(B):
                    for h in range(HG):
                        n, n0 = B * g + b, B * g0 + b
                        s = 4 * n + h
                        prev = not (first and b == 0 and h == 0)
                        pb_, ph_ = ((b - 1) % B if h == 0 else b), (h - 1) % HG
                        if prev:
                            p_lo(s - 1, 0)
                            p_lo(s - 1, 1)
                        for k, tiles in enumerate(SBANKS):
                            dve.wait_ge(s_sc, 3 * s + k + 1)
                            for i in tiles:
                                w = (i + 1) * P
                                ins = nc.vector.tensor_reduce(mn[:, h % 2, i:i + 1], SCf[:, SOFF[i]:SOFF[i] + w],
                                                              AX_X, ALU.min)
                            ins.then_inc(d_min, 1)
                        if prev:
                            p_lo(s - 1, 2)
                            p_lo(s - 1, 3)
                        qs, rest = tasks_of(n0, h)
                        for kind, m0, idx, bank in qs:
                            rope(kind, n + (m0 - n0), idx, m0, bank)
                        dve.wait_ge(a_exp, 3 * s + 3)
                        nc.vector.reciprocal(ri[:, h % 2, :], rs[:, h % 2, :]).then_inc(d_rec, 1)
                        dve.wait_ge(d_rec, s + 1)
                        for i in range(TB - 1, -1, -1):
                            pt = p[:, h % 2, SOFF[i]:SOFF[i] + (i + 1) * P]
                            ins = nc.vector.tensor_scalar(pt, pt, ri[:, h % 2, i:i + 1], PSCALE, ALU.mult, ALU.mult)
                        ins.then_inc(d_norm, 1)
                        if prev:
                            out_lo(s - 1, pb_, ph_)
                        for kind, m0, idx, bank in rest:
                            m = n + (m0 - n0)
                            if kind == "K":
                                rope(kind, m, idx, m0, bank)
                            if kind == "V":
                                value_lo(m, m0, bank)
                            if kind == "O":
                                project_add(m, idx, m0 % B, bank)
            bodies(dve, body)
            SL = G * B * HG
            for j in range(TB):
                p_lo(SL - 1, j)
            out_lo(SL - 1, B - 1, HG - 1)
            for kind, n, idx, bank in EPILOGUE:
                project_add(n, idx, n % B, bank)
            dve.wait_ge(o_add, 4 * G * B)

            layernorm(2, True)
            ffn(1)

        @block.tensor
        def _(pe):
            mm = nc.tensor.matmul

            def mm3(out_, lh, ll, rh, rl, start, stop):
                mm(out_, lh, rh, start=start, stop=False)
                mm(out_, lh, rl, start=False, stop=False)
                return mm(out_, ll, rh, start=False, stop=stop)

            pe.wait_ge(ld_f, 16 * NFL)
            mm(PV[0:RDIM, 0:NSLOT], fwrT[:, :], fkeyT[:, :], start=True, stop=True).then_inc(fs_pe, 1)
            pe.wait_ge(fs_ev, 1)
            mm(TR[0:BOT, 0, 0:NSLOT], fwr[:, :], rk[:, :], start=True, stop=True).then_inc(fs_pe, 1)
            for c in range(CC):
                ins = mm(SC[0:VB, 0, 0:NSLOT], fwvdT[:, c, :], fvalT[:, c, :], start=c == 0, stop=c == CC - 1)
            ins.then_inc(fs_pe, 2)
            pe.wait_ge(fs_ev, 2)
            for c in range(CC):
                if c >= 2:
                    pe.wait_ge(fs_lo, c)
                mm(PJ[:, c % 2, 0:NSLOT], fwq[:, c * P:(c + 1) * P], rmat[:, :], start=True, stop=True)
                mm(PJ[:, c % 2, NSLOT:2 * NSLOT], fwq[:, c * P:(c + 1) * P], fkeyT[:, :],
                   start=True, stop=True).then_inc(fs_pe, 1)
            pe.wait_ge(fs_ev, 3)
            mm(PV[:, :], u1T[:, :], fwvuT[:, :], start=True, stop=True).then_inc(fs_pe, 1)
            pe.wait_ge(cst, 1)

            def layernorm(k):
                if k > 0:
                    pe.wait_ge(ln_lo, NT * k)
                with pe.Fori(0, NT // 2) as m:
                    for i in range(2):
                        pe.wait_ge(ln_h, NT * k + 2 * m + i + 1)
                        for c in range(CC):
                            ins = nc.tensor.transpose(TR[:, i, c * P:(c + 1) * P], hbuf[:, i, c * P:(c + 1) * P],
                                                      ident[:, :])
                        ins.then_inc(ln_t, 1)

            def ffn(f):
                pe.wait_ge(ln_lo, NT * (2 * f + 1))
                pe.wait_ge(fs_lo, 6)
                for c in range(4):
                    if c >= 2:
                        pe.wait_ge(u_g, 4 * f + c - 1)
                    for k in range(CC):
                        xs = slice(c * T, (c + 1) * T)
                        ins = mm3(PJ[:, c % 2, :], uh[:, k, :], ul[:, k, :], XTh[:, k, xs], XTl[:, k, xs],
                                  k == 0, k == CC - 1)
                    ins.then_inc(u_ps, 1)
                    if c >= 1:
                        hidden_out(f, c - 1)
                hidden_out(f, 3)
                pe.wait_ge(g_sum, f + 1)
                mm(PV[:, NT:NT + 1], ones[:, :], lsum[:, :], start=True, stop=True).then_inc(g_ps, 1)

                def score(c):
                    if c >= 2:
                        pe.wait_ge(r_use, 8 * f + 2 * (c - 2) + 2)
                    elif c == 1:
                        pe.wait_ge(u_g, 4 * f + 4)
                    for i in range(TB):
                        n = 4 * c + i
                        bank = (SC if c % 2 == 0 else PJ)[:, i // 2, (i % 2) * 2 * NSLOT:(i % 2 + 1) * 2 * NSLOT]
                        for k in range(CC):
                            xs = slice(n * P, (n + 1) * P)
                            lh, ll = XTh[:, k, xs], XTl[:, k, xs]
                            ins = mm3(bank, lh, ll, ah[:, k, :], al[:, k, :], k == 0, k == CC - 1)
                        if i % 2:
                            ins.then_inc(r_sc, 1)

                score(0)
                for c in range(4):
                    if c < 3:
                        score(c + 1)
                    pe.wait_ge(r_e, 4 * f + c + 1)
                    if c >= 1:
                        pe.wait_ge(r_lo, 4 * f + c)
                    for i in range(TB):
                        ins = nc.tensor.transpose(TR[:, 0, i * P:(i + 1) * P], ee[:, c % 2, i, :], ident[:, :])
                    ins.then_inc(r_t, 1)
                    pe.wait_ge(r_lo, 4 * f + c + 1)
                    for i in range(TB):
                        n = 4 * c + i
                        bank = SC[:, 2, :] if i % 2 == 0 else PV[:, :]
                        if n >= 2:
                            pe.wait_ge(r_x, NT * f + n - 1)
                        else:
                            pe.wait_ge(g_ex, 2 * f + 2)
                        ts = slice(i * P, (i + 1) * P)
                        mm3(bank, eTh[:, ts], eTl[:, ts], v2h[:, :], v2l[:, :], True, True).then_inc(r_aux, 1)

            def hidden_out(f, c):
                pe.wait_ge(u_g, 4 * f + c + 1)
                for i in range(TB):
                    n = 4 * c + i
                    ins = mm(PV[:, n:n + 1], gT[:, c % 2, i * P:(i + 1) * P], wu2T[:, :], start=True, stop=True)
                ins.then_inc(u_l, 1)

            layernorm(0)
            ffn(0)
            layernorm(1)

            def proj(kind, n, idx, n0, bank):
                b, g0 = n0 % B, n0 // B
                g = (n - b) // B if isinstance(n, int) else None
                before = BEFORE[(kind, n0, idx)]
                if before:
                    bk, bn, bi, _ = before
                    pe.wait_ge(*consumed(bk, n + (bn - n0), bi, bn))
                if kind in "QKV":
                    k = PIECES.index(kind + (str(idx) if kind == "Q" else ""))
                    return b, k
                return b, None

            def project(kind, n, idx, n0, bank, g):
                b, k = proj(kind, n, idx, n0, bank)
                xs = slice(b * T, (b + 1) * T)
                out_ = PJ[:, bank, :]
                if kind in "QK":
                    pe.wait_ge(w_lo, NPC * g + k + 1)
                    for c in range(CC):
                        ins = mm3(out_, wh[:, k, c, :], wl[:, k, c, :], XTh[:, c, xs], XTl[:, c, xs],
                                  c == 0, c == CC - 1)
                    ins.then_inc(s_q if kind == "Q" else s_k, 1)
                elif kind == "V":
                    pe.wait_ge(w_lo, NPC * g + k + 1)
                    for t in range(TB):
                        ts = slice(b * T + t * P, b * T + (t + 1) * P)
                        for c in range(CC):
                            ins = mm3(out_[:, t * D:(t + 1) * D], XTh[:, c, ts], XTl[:, c, ts],
                                      wh[:, k, c, :], wl[:, k, c, :], c == 0, c == CC - 1)
                    ins.then_inc(s_v, 1)
                else:
                    if idx == 0:
                        pe.wait_ge(o_lo, 4 * n + 4)
                        pe.wait_ge(wo_lo, HG * g + HG)
                    ts = slice(idx * P, (idx + 1) * P)
                    for h in range(HG):
                        ins = mm3(out_, oTh[:, b % 2, h, ts], oTl[:, b % 2, h, ts], woh[:, h, :], wol[:, h, :],
                                  h == 0, h == HG - 1)
                    ins.then_inc(s_o, 1)

            def transposed(s, s0, j):
                if j == 0:
                    pe.wait_ge(d_norm, s + 1)
                if s0 > 0 or j >= 2:
                    pe.wait_ge(tr_lo, 4 * s + j - 1)
                else:
                    pe.wait_ge(ln_lo, 2 * NT)
                for i in range(j, TB):
                    ins = nc.tensor.transpose(TR[:, j % 2, (i - j) * P:(i - j + 1) * P],
                                              p[:, s0 % 2, SOFF[i] + j * P:SOFF[i] + (j + 1) * P], ident[:, :])
                ins.then_inc(s_tr, 1)

            def attend(s, s0, j):
                pe.wait_ge(tr_lo, 4 * s + j + 1)
                if j == 0:
                    if s0 > 0:
                        pe.wait_ge(o_lo, s)
                par = (s0 // 4) % 2
                w = (TB - j) * P
                ins = mm3(PV[:, j * P:T], vh[:, par, j, :], vl[:, par, j, :], pTh[:, TOFF[j]:TOFF[j] + w],
                          pTl[:, TOFF[j]:TOFF[j] + w], j == 0, j == TB - 1)
                if j == TB - 1:
                    ins.then_inc(s_pv, 1)

            def scores(s, s0, n, n0, h):
                pe.wait_ge(rope_lo, rope_index("Q", n, h, n0) + 1)
                for k, tiles in enumerate(SBANKS):
                    if s0 > 0:
                        pe.wait_ge(a_exp, 3 * s + k - 2)
                    for i in tiles:
                        w = (i + 1) * P
                        ts = slice(i * P, w)
                        o = SCf[:, SOFF[i]:SOFF[i] + w]
                        qh, ql, kh, kl = (qTh[:, h, ts], qTl[:, h, ts], kTh[:, n0 % 2, 0:w], kTl[:, n0 % 2, 0:w])
                        mm(o, qh, kh, start=True, stop=False)
                        mm(o, qh, kl, start=False, stop=False)
                        mm(o, ql, kh, start=False, stop=False)
                        ins = mm(SCf[:, SOFF[i] + w - P:SOFF[i] + w], identb[:, :], maskb[:, :],
                                 start=False, stop=True)
                    ins.then_inc(s_sc, 1)

            pe.wait_ge(ln_lo, 2 * NT)
            for kind, n, idx, bank in PROLOGUE:
                if kind == "V":
                    pass
                project(kind, n, idx, n, bank, 0)
            pe.wait_ge(v_lo, 1)

            def body(g, first, last):
                g0 = rep(g, first, last)
                for b in range(B):
                    for h in range(HG):
                        n, n0 = B * g + b, B * g0 + b
                        s, s0 = 4 * n + h, 4 * n0 + h
                        prev = s0 > 0

                        def run(tasks):
                            for kind, m0, idx, bank in tasks:
                                project(kind, n + (m0 - n0), idx, m0, bank, g + (m0 // B - g0))
                        if prev:
                            transposed(s - 1, s0 - 1, 0)
                            transposed(s - 1, s0 - 1, 1)
                        scores(s, s0, n, n0, h)
                        if prev:
                            if h == 1:
                                pe.wait_ge(v_lo, n + 1)
                            attend(s - 1, s0 - 1, 0)
                            transposed(s - 1, s0 - 1, 2)
                            attend(s - 1, s0 - 1, 1)
                            transposed(s - 1, s0 - 1, 3)
                        qs, rest = tasks_of(n0, h)
                        run(qs)
                        if prev:
                            attend(s - 1, s0 - 1, 2)
                            attend(s - 1, s0 - 1, 3)
                        run(rest)
            bodies(pe, body)
            SL = G * B * HG
            transposed(SL - 1, SL - 1, 0)
            transposed(SL - 1, SL - 1, 1)
            attend(SL - 1, SL - 1, 0)
            transposed(SL - 1, SL - 1, 2)
            attend(SL - 1, SL - 1, 1)
            transposed(SL - 1, SL - 1, 3)
            attend(SL - 1, SL - 1, 2)
            attend(SL - 1, SL - 1, 3)
            for kind, n, idx, bank in EPILOGUE:
                project(kind, n, idx, n, bank, G - 1)

            layernorm(2)
            ffn(1)


NFL = 19
SPLIT_AT = {(2, 1): [0], (2, 3): [1], (3, 0): [2, 3], (3, 1): [4], (3, 2): [5]}


def kernel(**inputs):
    import numpy as np
    import concourse.bacc as bacc
    from concourse.bass_utils import run_bass_kernel_spmd

    a = {k: np.asarray(v) for k, v in inputs.items()}
    perm = np.concatenate([np.arange(0, D, 2), np.arange(1, D, 2)])
    wq = a["L0_attn_Wq"].reshape(CC, P, G, HG, D)[..., perm].transpose(2, 1, 3, 0, 4)
    wk = a["L0_attn_Wk"].reshape(CC, P, G, D)[..., perm].transpose(2, 1, 0, 3)
    wv = a["L0_attn_Wv"].reshape(CC, P, G, D).transpose(2, 1, 0, 3)
    parts = {"K": wk, "V": wv, **{f"Q{h}": wq[:, :, h] for h in range(HG)}}
    wqkv = np.stack([parts[k] for k in PIECES], axis=2)
    wo = a["L0_attn_Wo"].reshape(G, HG, D, C).transpose(0, 2, 1, 3)
    freqs = (1.0 / np.float32(10000.0) ** (np.arange(0, D, 2, dtype=np.float32) / np.float32(D))).astype(np.float32)
    angle = np.arange(T, dtype=np.float32)[None, :] * freqs[:, None]
    cos, sin = np.cos(angle), np.sin(angle)
    cosk, sink = np.concatenate([cos, cos]), np.concatenate([-sin, sin])
    arrays = {
        "x": a["L0_attn_x"].reshape(B * T, C), "wqkv": wqkv, "wo": wo, "bo": a["L0_attn_bo"].reshape(1, C),
        "cosq": cosk * np.float32(-SCALE), "sinq": sink * np.float32(-SCALE), "cosk": cosk, "sink": sink,
        "f_wq": a["L0_ffn_Wq"], "f_wr": a["L0_ffn_Wr"], "f_wrT": a["L0_ffn_Wr"].T,
        "f_keyT": a["L0_ffn_aux_keys"].T, "f_valT": a["L0_ffn_aux_values"].T, "f_wvdT": a["L0_ffn_Wvd"].T,
        "f_wvuT": a["L0_ffn_Wvu"].T, "f_wu1T": a["L0_ffn_Wu1"].T, "f_bu1": a["L0_ffn_bu1"].reshape(P, 1),
        "f_wu2T": a["L0_ffn_Wu2"].T, "f_bu2": a["L0_ffn_bu2"].reshape(1, 1),
        "f_gw": a["L0_ffn_gate_w1"].reshape(1, 1), "f_gb": a["L0_ffn_gate_bias"].reshape(1, 1),
        "f_lr": a["L0_ffn_log_rel"].reshape(1, NSLOT),
    }
    arrays = {k: np.ascontiguousarray(v) for k, v in arrays.items()}
    nc = bacc.Bacc("TRN2", target_bir_lowering=False, num_devices=1)
    args = [nc.dram_tensor(f"in_{k}", v.shape, mybir.dt.from_np(v.dtype), kind="ExternalInput").ap()
            for k, v in arrays.items()]
    out = nc.dram_tensor("out_0", (B * T, C), F32, kind="ExternalOutput").ap()
    macaron_kernel(nc, *args, out)
    r = run_bass_kernel_spmd(nc, [{f"in_{k}": v for k, v in arrays.items()}], core_ids=[0])
    return r.results[0]["out_0"].reshape(B, T, C)
```

```python
from contextlib import ExitStack

import concourse.bass as bass
from concourse import mybir

ALU = mybir.AluOpType
ACT = mybir.ActivationFunctionType
F32 = mybir.dt.float32
BF16 = mybir.dt.bfloat16
F16 = mybir.dt.float16
AX_X = mybir.AxisListType.X

P = 128
B, T, C = 4, 512, 512
NT = B * T // P
TB = T // P
CC = C // P
G, HG, D = 8, 4, 128
SCALE = float(D) ** -0.5
BOT, RDIM, NSLOT, VB = 64, 48, 128, 32
EPS = 1e-5
TAU_LOW, TAU_HIGH, EARLY_EXIT = 0.5, 2.0, 0.05
PSCALE = 1024.0
MASKED = 1e30
SELECTED = -3e38
SOFF = [896, 1024, 512, 0]
SBANKS = [[3], [2, 0], [1]]
TOFF = [0, 512, 896, 1152]
NP_ = 1280
PIECES = ["K", "Q0", "Q1", "V", "Q2", "Q3"]
NPC = len(PIECES)


def macaron_kernel(nc: bass.Bass, x, wqkv, wo, bo, cosq, sinq, cosk, sink,
                   f_wq, f_wr, f_wrT, f_keyT, f_valT, f_wvdT, f_wvuT, f_wu1T, f_bu1, f_wu2T,
                   f_bu2, f_gw, f_gb, f_lr, out):
    ctx = ExitStack()
    with ctx:
        def sb(name, shape, dt):
            return ctx.enter_context(nc.sbuf_tensor(name, shape, dt))

        def pb(name, shape, dt):
            return ctx.enter_context(nc.psum_tensor(name, shape, dt))

        def sem(name):
            return ctx.enter_context(nc.semaphore(name))

        X = sb("X", [P, NT, C], F32)
        XTh = sb("XTh", [P, CC, B * T], F16)
        XTl = sb("XTl", [P, CC, B * T], F16)
        cq, sq = sb("cq", [P, T], F32), sb("sq", [P, T], F32)
        ck, sk = sb("ck", [P, T], F32), sb("sk", [P, T], F32)
        wraw = sb("wraw", [P, NPC, CC, D], F32)
        wh = sb("wh", [P, NPC, CC, D], BF16)
        wl = sb("wl", [P, NPC, CC, D], F16)
        woraw = sb("woraw", [P, HG, C], F32)
        woh = sb("woh", [P, HG, C], BF16)
        wol = sb("wol", [P, HG, C], F16)
        kTh, kTl = sb("kTh", [P, 2, T], BF16), sb("kTl", [P, 2, T], F16)
        vh, vl = sb("vh", [P, 2, TB, D], BF16), sb("vl", [P, 2, TB, D], F16)
        qTh, qTl = sb("qTh", [P, HG, T], BF16), sb("qTl", [P, HG, T], F16)
        t1, t2 = sb("t1", [P, NROPE, T], F32), sb("t2", [P, NROPE, T], F32)
        p = sb("p", [P, 2, NP_], F32)
        pTh, pTl = sb("pTh", [P, NP_], F16), sb("pTl", [P, NP_], F16)
        oTh, oTl = sb("oTh", [P, 2, HG, T], BF16), sb("oTl", [P, 2, HG, T], F16)
        mn, rs, ri = sb("mn", [P, 2, TB], F32), sb("rs", [P, 2, TB], F32), sb("ri", [P, 2, TB], F32)
        ident = sb("ident", [P, P], F32)
        identb = sb("identb", [P, P], BF16)
        maskb = sb("maskb", [P, P], BF16)
        ones = sb("ones", [P, P], F32)
        bob = sb("bob", [P, C], F32)
        st = sb("st", [P, NT, 6], F32)
        mv = sb("mv", [P, NT, 2], F32)
        ve, sd, rstd, nw = (sb(n, [P, NT], F32) for n in ("ve", "sd", "rstd", "nw"))
        hbuf = sb("hbuf", [P, 4, C], F32)
        fwq = sb("fwq", [BOT, C], F32)
        fwr, fwrT = sb("fwr", [RDIM, BOT], F32), sb("fwrT", [BOT, RDIM], F32)
        fkeyT = sb("fkeyT", [BOT, NSLOT], F32)
        fvalT, fwvdT = sb("fvalT", [P, CC, NSLOT], F32), sb("fwvdT", [P, CC, VB], F32)
        fwvuT = sb("fwvuT", [VB, C], F32)
        fwu1T = sb("fwu1T", [P, CC, P], F32)
        bu1, wu2T = sb("bu1", [P, 1], F32), sb("wu2T", [P, 1], F32)
        bu2, gw, gb = sb("bu2", [P, 1], F32), sb("gw", [P, 1], F32), sb("gb", [P, 1], F32)
        lrb = sb("lrb", [P, NSLOT], F32)
        rk = sb("rk", [RDIM, NSLOT], F32)
        rmat = sb("rmat", [BOT, NSLOT], F32)
        u1T = sb("u1T", [VB, NSLOT], F32)
        ah, al = sb("ah", [P, CC, 2 * NSLOT], BF16), sb("al", [P, CC, 2 * NSLOT], F16)
        v2h, v2l = sb("v2h", [P, C], BF16), sb("v2l", [P, C], F16)
        uh, ul = sb("uh", [P, CC, P], BF16), sb("ul", [P, CC, P], F16)
        gT = t2
        lv, lsum = sb("lv", [P, NT], F32), sb("lsum", [P, 1], F32)
        gt, gt2, gt3, gate = (sb(n, [P, NT], F32) for n in ("gt", "gt2", "gt3", "gate"))
        rsc = t1[:, 0, :].rearrange("p (t n) -> p t n", t=TB)
        mr = t1[:, 1:3, :].rearrange("p m (t n) -> p m t n", t=TB)
        asc = p[:, :, :].rearrange("p m n -> p (m n)")[:, 0:B * T].rearrange("p (t n) -> p t n", t=NT)
        m8 = sb("m8", [P, TB, 8], F32)
        mnr, sm, gs = sb("mnr", [P, NT], F32), sb("sm", [P, NT], F32), sb("gs", [P, NT], F32)
        xa, xb = sb("xa", [P, NT], F32), sb("xb", [P, NT], F32)
        eTh = pTh[:, 0:2 * T].rearrange("p (m t) -> p m t", m=2)
        eTl = pTl[:, 0:2 * T].rearrange("p (m t) -> p m t", m=2)

        PJ = pb("PJ", [P, 2, T], F32)
        SC = pb("SC", [P, 3, T], F32)
        TR = pb("TR", [P, 2, T], F32)
        PV = pb("PV", [P, T], F32)
        SCf = SC[:, :, :].rearrange("p b n -> p (b n)")

        ld_x = [sem(f"ld_x{i}") for i in range(4)]
        ld_f = sem("ld_f")
        ld_t = sem("ld_t")
        ld_w = sem("ld_w")
        ld_wo = sem("ld_wo")
        st_out = sem("st_out")
        cst0, cst = sem("cst0"), sem("cst")
        dch = sem("dch")
        fs_pe, fs_ev = sem("fs_pe"), sem("fs_ev")
        fs_hi, fs_lo = sem("fs_hi"), sem("fs_lo")
        ln_m = sem("ln_m")
        ln_v, ln_sd = sem("ln_v"), sem("ln_sd")
        ln_h, ln_t = sem("ln_h"), sem("ln_t")
        ln_hi, ln_lo = sem("ln_hi"), sem("ln_lo")
        bo_add = sem("bo_add")
        u_ps, u_g, u_l = sem("u_ps"), sem("u_g"), sem("u_l")
        g_lv, g_sum, g_ps = sem("g_lv"), sem("g_sum"), sem("g_ps")
        g_ex, g_exd = sem("g_ex"), sem("g_exd")
        r_sc, r_use = sem("r_sc"), sem("r_use")
        r_pen, r_am = sem("r_pen"), sem("r_am")
        r_mn, r_e = sem("r_mn"), sem("r_e")
        r_t, r_hi, r_lo = sem("r_t"), sem("r_hi"), sem("r_lo")
        r_aux, r_gs = sem("r_aux"), sem("r_gs")
        r_xd = sem("r_xd")
        r_xa, r_xp = sem("r_xa"), sem("r_xp")
        x_ab, x_up = sem("x_ab"), sem("x_up")
        w_hi, w_lo = sem("w_hi"), sem("w_lo")
        wo_hi, wo_lo = sem("wo_hi"), sem("wo_lo")
        s_q, s_k, s_v, s_o = sem("s_q"), sem("s_k"), sem("s_v"), sem("s_o")
        rope_mul, rope_sum = sem("rope_mul"), sem("rope_sum")
        rope_hi, rope_lo = sem("rope_hi"), sem("rope_lo")
        v_hi, v_lo = sem("v_hi"), sem("v_lo")
        s_sc, d_min, a_exp = sem("s_sc"), sem("d_min"), sem("a_exp")
        d_norm = sem("d_norm")
        s_tr, tr_hi, tr_lo = sem("s_tr"), sem("tr_hi"), sem("tr_lo")
        s_pv, o_hi, o_lo = sem("s_pv"), sem("o_hi"), sem("o_lo")
        o_add = sem("o_add")

        def turn_bank(i):
            return (TR if i < 2 else PJ)[:, i % 2, :]

        def score_bank(c, j):
            return SC[:, j, :] if c % 2 == 0 else (PJ[:, 1, :], SC[:, 2, :])[j]

        x_v = x.rearrange("(n p) c -> p n c", p=P)
        out_v = out.rearrange("(n p) c -> p n c", p=P)

        def tasks_of(n, h):
            q = [("Q", n, h + 2, 0)] if h < 2 else [("Q", n + 1, h - 2, 3 - h)]
            rest = {0: [("K", n + 1, 0, 1)],
                    1: [("O", n - 1, 0, 1), ("O", n - 1, 1, 0)],
                    2: [("V", n + 1, 0, 0), ("O", n - 1, 2, 1)],
                    3: [("O", n - 1, 3, 1)]}[h]
            ok = lambda t: 0 <= t[1] < G * B
            return [t for t in q if ok(t)], [t for t in rest if ok(t)]

        PROLOGUE = [("K", 0, 0, 0), ("V", 0, 0, 1), ("Q", 0, 0, 1), ("Q", 0, 1, 0)]
        EPILOGUE = [("O", G * B - 1, i, (i + 1) % 2) for i in range(TB)]
        ALL = list(PROLOGUE)
        for n_ in range(G * B):
            for h_ in range(HG):
                a_, b_ = tasks_of(n_, h_)
                ALL += a_ + b_
        ALL += EPILOGUE
        BEFORE, last_of = {}, {}
        for t_ in ALL:
            BEFORE[t_[:3]] = last_of.get(t_[3])
            last_of[t_[3]] = t_

        def rope_index(kind, n, idx, n0):
            if kind == "K":
                return 0 if n0 == 0 else 5 * n - 1
            return 5 * n + (1, 2, 3, 5 if n0 < G * B - 1 else 4)[idx]

        def consumed(kind, n, idx, n0):
            if kind in "QK":
                return rope_mul, rope_index(kind, n, idx, n0) + 1
            if kind == "V":
                return v_lo, n + 1
            return o_add, 4 * n + idx + 1

        def rep(g, first, last):
            return 0 if first else (G - 1 if last else 3)

        def bodies(eng, body):
            body(0, True, False)
            with eng.Fori(1, G - 1) as g:
                body(g, False, False)
            body(G - 1, False, True)

        block = ctx.enter_context(nc.Block())

        @block.sync
        def _(sp):
            fl = [(fwq[:, :], f_wq), (fwr[:, :], f_wr), (fwrT[:, :], f_wrT), (fkeyT[:, :], f_keyT),
                  (fvalT[:, :, :], f_valT.rearrange("(c p) n -> p c n", p=P)),
                  (fwvdT[:, :, :], f_wvdT.rearrange("(c p) n -> p c n", p=P)),
                  (fwvuT[:, :], f_wvuT), (fwu1T[:, :, :], f_wu1T.rearrange("(c p) n -> p c n", p=P)),
                  (bu1[:, :], f_bu1), (wu2T[:, :], f_wu2T),
                  (bu2[:, :], f_bu2.to_broadcast([P, 1])), (gw[:, :], f_gw.to_broadcast([P, 1])),
                  (gb[:, :], f_gb.to_broadcast([P, 1])), (lrb[:, :], f_lr.to_broadcast([P, NSLOT]))]
            assert len(fl) == NFL
            for dst, src in fl:
                sp.dma_start(dst, src).then_inc(ld_f, 16)
            for dst, src in ((bob[:, :], bo.to_broadcast([P, C])), (cq[:, :], cosq), (sq[:, :], sinq),
                             (ck[:, :], cosk), (sk[:, :], sink)):
                sp.dma_start(dst, src).then_inc(ld_t, 16)
            sp.dma_start(wraw[:, :, :, :], wqkv[0]).then_inc(ld_w, 16)
            sp.dma_start(woraw[:, :, :], wo[0]).then_inc(ld_wo, 16)

            def body(g, first, last):
                if not last:
                    sp.wait_ge(w_lo, NPC * g + NPC)
                    sp.dma_start(wraw[:, :, :, :], wqkv[g + 1]).then_inc(ld_w, 16)
                    sp.wait_ge(wo_lo, HG * g + HG)
                    sp.dma_start(woraw[:, :, :], wo[g + 1]).then_inc(ld_wo, 16)
            bodies(sp, body)
            for i in range(4):
                sp.wait_ge(r_xd, NT // 2 + 2 * i + 2)
                sp.wait_ge(r_xp, NT // 2 + 2 * i + 2)
                sp.dma_start(out_v[:, 4 * i:4 * i + 4, :], X[:, 4 * i:4 * i + 4, :]).then_inc(st_out, 16)
            sp.wait_ge(st_out, 64)

        @block.gpsimd
        def _(pool):
            nc.gpsimd.memset(ident[:, :], 0.0)
            nc.gpsimd.memset(identb[:, :], 0.0)
            nc.gpsimd.memset(maskb[:, :], 0.0)
            nc.gpsimd.memset(ones[:, :], 1.0).then_inc(cst0, 1)
            pool.wait_ge(cst0, 1)
            for m in (ident, identb):
                nc.gpsimd.affine_select(out=m[:, :], in_=m[:, :], compare_op=ALU.not_equal, fill=1.0,
                                        base=0, pattern=[[-1, P]], channel_multiplier=1)
            nc.gpsimd.affine_select(out=maskb[:, :], in_=maskb[:, :], compare_op=ALU.is_ge, fill=MASKED,
                                    base=0, pattern=[[-1, P]], channel_multiplier=1).then_inc(cst, 1)

            def ffn(f):
                for c in range(4):
                    pool.wait_ge(r_pen, 4 * f + c + 1)
                    a4 = asc[:, 4 * c:4 * c + 4, :]
                    nc.gpsimd.tensor_tensor(a4, a4, mr[:, c % 2, :, :], ALU.add).then_inc(r_am, 1)
                for n in range(1, NT, 2):
                    pool.wait_ge(r_xa, 8 * f + n // 2 + 1)
                    nc.gpsimd.tensor_tensor(X[:, n, :], X[:, n, :], hbuf[:, n // 2 % 2, :],
                                            ALU.add).then_inc(r_xp, 1)

            ffn(0)
            pool.wait_ge(ld_t, 80)
            for n in range(NT):
                pool.wait_ge(ln_h, NT + n + 1)
                nc.gpsimd.tensor_tensor(X[:, n, :], X[:, n, :], bob[:, :], ALU.add).then_inc(bo_add, 1)

            def w_low(g, k):
                pool.wait_ge(w_hi, NPC * g + k + 1)
                nc.gpsimd.tensor_tensor(wl[:, k, :, :], wraw[:, k, :, :], wh[:, k, :, :],
                                        ALU.subtract).then_inc(w_lo, 1)

            def rope(kind, n, idx, n0, par):
                r = rope_index(kind, n, idx, n0)
                j = rope_index(kind, n0, idx, n0) % NROPE
                pool.wait_ge(rope_mul, r + 1)
                nc.gpsimd.tensor_tensor(t1[:, j, :], t1[:, j, :], t2[:, j, :], ALU.add).then_inc(rope_sum, 1)
                pool.wait_ge(rope_hi, r + 1)
                hi, lo = (qTh[:, idx, :], qTl[:, idx, :]) if kind == "Q" else (kTh[:, par, :], kTl[:, par, :])
                nc.gpsimd.tensor_tensor(lo, t1[:, j, :], hi, ALU.subtract).then_inc(rope_lo, 1)

            for k in range(NPC):
                w_low(0, k)
            for kind, n, idx, _ in PROLOGUE:
                if kind in "QK":
                    rope(kind, n, idx, n, n % 2)

            def body(g, first, last):
                g0 = rep(g, first, last)
                for b in range(B):
                    for h in range(HG):
                        n, n0 = B * g + b, B * g0 + b
                        if b == 1 and h == 0:
                            for k in range(HG):
                                pool.wait_ge(wo_hi, HG * g + k + 1)
                                nc.gpsimd.tensor_tensor(wol[:, k, :], woraw[:, k, :], woh[:, k, :],
                                                        ALU.subtract).then_inc(wo_lo, 1)
                        qs, rest = tasks_of(n0, h)
                        for kind, m0, idx, _ in qs + rest:
                            if kind in "QK":
                                rope(kind, n + (m0 - n0), idx, m0, m0 % 2)
                        if not last:
                            for k in SPLIT_AT.get((b, h), []):
                                w_low(g + 1, k)
            bodies(pool, body)
            ffn(1)

        @block.scalar
        def _(act):
            for i in range(4):
                act.dma_start(X[:, 4 * i:4 * i + 4, :], x_v[:, 4 * i:4 * i + 4, :]).then_inc(ld_x[i], 16)
            act.wait_ge(ld_f, 16 * NFL)
            nc.scalar.copy(uh[:, :, :], fwu1T[:, :, :]).then_inc(fs_hi, 1)
            for c in range(CC):
                act.wait_ge(fs_pe, 5 + c)
                nc.scalar.copy(ah[:, c, :], PJ[:, c % 2, 0:2 * NSLOT]).then_inc(fs_hi, 1)
            act.wait_ge(fs_pe, 9)
            nc.scalar.copy(v2h[:, :], PV[:, :]).then_inc(fs_hi, 1)

            def roots(k):
                act.wait_ge(ln_v, k + 1)
                nc.scalar.activation(sd[:, :], ve[:, :], ACT.Sqrt).then_inc(ln_sd, 1)

            def layernorm(k):
                roots(k)
                with act.Fori(0, NT // 4) as m:
                    for i in range(4):
                        act.wait_ge(ln_t, NT * k + 4 * m + i + 1)
                        nc.scalar.copy(XTh[:, :, bass.ds(m * 4 * P + i * P, P)],
                                       turn_bank(i).rearrange("p (c t) -> p c t", c=CC)).then_inc(ln_hi, 1)

            def ffn(f):
                k = 2 * f

                def gelu(c):
                    act.wait_ge(u_ps, 4 * f + c + 1)
                    if 4 * f + c >= 2:
                        act.wait_ge(u_l, 4 * f + c - 1)
                    nc.scalar.activation(gT[:, c % 2, :], PJ[:, 0, :], ACT.Gelu_apprx_tanh,
                                         bias=bu1[:, 0:1]).then_inc(u_g, 1)

                roots(k)
                for c in range(4):
                    for n in range(4 * c, 4 * c + 4):
                        act.wait_ge(ln_t, NT * k + n + 1)
                        nc.scalar.copy(XTh[:, :, n * P:(n + 1) * P],
                                       TR[:, n % 2, :].rearrange("p (c t) -> p c t", c=CC)).then_inc(ln_hi, 1)
                        if n == 0:
                            act.wait_ge(x_ab, f + 1)
                        nc.scalar.activation(X[:, n, :], X[:, n, :], ACT.Identity, bias=xb[:, n:n + 1],
                                             scale=xa[:, n:n + 1]).then_inc(x_up, 1)
                    if c:
                        gelu(c - 1)
                gelu(3)
                act.wait_ge(g_lv, 2 * f + 1)
                nc.scalar.activation(lv[:, :], gt[:, :], ACT.Ln, bias=1.0).then_inc(g_lv, 1)

                def exps(c):
                    act.wait_ge(r_mn, 4 * f + c + 1)
                    for n in range(4 * c, 4 * c + 4):
                        ins = nc.scalar.activation(asc[:, n, :], asc[:, n, :], ACT.Exp, bias=mnr[:, n:n + 1],
                                                   scale=-1.0, accum_out=sm[:, n:n + 1])
                    ins.then_inc(r_e, 1)
                exps(0)
                exps(1)
                for j in range(2):
                    act.wait_ge(g_ex, 2 * f + j + 1)
                    nc.scalar.activation(gt2[:, :], gt[:, :], ACT.Exp, scale=-1.0).then_inc(g_exd, 1)

                def turned(c):
                    act.wait_ge(r_t, 4 * f + c + 1)
                    nc.scalar.copy(eTh[:, c % 2, :], TR[:, c % 2, :]).then_inc(r_hi, 1)
                turned(0)
                for c in range(4):
                    if c < 2:
                        exps(c + 2)
                    if c < 3:
                        turned(c + 1)
                    for n in (4 * c + 1, 4 * c + 3):
                        act.wait_ge(r_aux, NT * f + n + 1)
                        act.wait_ge(r_gs, 4 * f + c + 1)
                        if n >= 5:
                            act.wait_ge(r_xp, 8 * f + n // 2 - 1)
                        nc.scalar.activation(hbuf[:, n // 2 % 2, :], PJ[:, 0, :], ACT.Copy,
                                             scale=gs[:, n:n + 1]).then_inc(r_xa, 1)

            ffn(0)
            layernorm(1)

            def w_high(g, k, wait):
                act.wait_ge(ld_w, 16 * g + 16)
                if wait:
                    act.wait_ge(*wait)
                nc.scalar.copy(wh[:, k, :, :], wraw[:, k, :, :]).then_inc(w_hi, 1)

            def rope(kind, n, idx, n0, par):
                r = rope_index(kind, n, idx, n0)
                j = rope_index(kind, n0, idx, n0) % NROPE
                act.wait_ge(rope_sum, r + 1)
                hi = qTh[:, idx, :] if kind == "Q" else kTh[:, par, :]
                nc.scalar.copy(hi, t1[:, j, :]).then_inc(rope_hi, 1)

            def value_hi(n, n0, bank):
                act.wait_ge(s_v, n + 1)
                nc.scalar.copy(vh[:, n0 % 2, :, :],
                               PJ[:, bank, :].rearrange("p (a d) -> p a d", a=TB)).then_inc(v_hi, 1)

            def p_hi(s, j):
                act.wait_ge(s_tr, 4 * s + j + 1)
                w = (TB - j) * P
                nc.scalar.copy(pTh[:, TOFF[j]:TOFF[j] + w], TR[:, j % 2, 0:w]).then_inc(tr_hi, 1)

            def out_hi(s, b, h):
                act.wait_ge(s_pv, s + 1)
                nc.scalar.mul(oTh[:, b % 2, h, :], PV[:, :], 1.0 / PSCALE).then_inc(o_hi, 1)

            for k in range(NPC):
                w_high(0, k, None)
            for kind, n, idx, bank in PROLOGUE:
                if kind in "QK":
                    rope(kind, n, idx, n, n % 2)
                if kind == "V":
                    value_hi(n, n, bank)

            def body(g, first, last):
                g0 = rep(g, first, last)
                for b in range(B):
                    for h in range(HG):
                        n, n0 = B * g + b, B * g0 + b
                        s = 4 * n + h
                        prev = not (first and b == 0 and h == 0)
                        pb_, ph_ = ((b - 1) % B if h == 0 else b), (h - 1) % HG
                        if prev:
                            p_hi(s - 1, 0)
                            p_hi(s - 1, 1)
                        for k, tiles in enumerate(SBANKS):
                            act.wait_ge(d_min, 3 * s + k + 1)
                            for i in tiles:
                                w = (i + 1) * P
                                ins = nc.scalar.activation(
                                    p[:, h % 2, SOFF[i]:SOFF[i] + w], SCf[:, SOFF[i]:SOFF[i] + w], ACT.Exp,
                                    bias=mn[:, h % 2, i:i + 1], scale=-1.0, accum_out=rs[:, h % 2, i:i + 1])
                            ins.then_inc(a_exp, 1)
                        if prev:
                            p_hi(s - 1, 2)
                            p_hi(s - 1, 3)
                            qs, rest = tasks_of(n0 if h else n0 - 1, ph_)
                            for kind, m0, idx, _ in qs + rest:
                                if kind in "QK":
                                    rope(kind, n + (m0 - n0), idx, m0, m0 % 2)
                        if b == 1 and h == 0:
                            act.wait_ge(ld_wo, 16 * g + 16)
                            if not first:
                                act.wait_ge(s_o, 16 * g)
                            for k in range(HG):
                                nc.scalar.copy(woh[:, k, :], woraw[:, k, :]).then_inc(wo_hi, 1)
                        if prev:
                            out_hi(s - 1, pb_, ph_)
                        for kind, m0, idx, bank in tasks_of(n0, h)[1]:
                            if kind == "V":
                                value_hi(n + (m0 - n0), m0, bank)
                        if not last:
                            for k in SPLIT_AT.get((b, h), []):
                                pc = PIECES[k]
                                reader = {"K": (s_k, 4 * g + 4), "V": (s_v, 4 * g + 4)}.get(
                                    pc, (s_q, 16 * g + 12 + int(pc[1:] or 0) + 1 if pc[0] == "Q" else 0))
                                w_high(g + 1, k, reader)
            bodies(act, body)
            SL = G * B * HG
            for j in range(TB):
                p_hi(SL - 1, j)
            out_hi(SL - 1, B - 1, HG - 1)

            ffn(1)

        @block.vector
        def _(dve):
            chain = [0]

            def link(ins):
                chain[0] += 1
                ins.then_inc(dch, 1)
                dve.wait_ge(dch, chain[0])

            def moments(n):
                return nc.vector.bn_stats(st[:, n, :], X[:, n, :]).then_inc(ln_m, 1)

            for n in range(NT):
                if n % 4 == 0:
                    dve.wait_ge(ld_x[n // 4], 16)
                moments(n)
            dve.wait_ge(fs_pe, 1)
            nc.vector.tensor_copy(rk[:, :], PV[0:RDIM, 0:NSLOT]).then_inc(fs_ev, 1)
            dve.wait_ge(fs_pe, 2)
            nc.vector.tensor_copy(rmat[:, :], TR[0:BOT, 0, 0:NSLOT]).then_inc(fs_ev, 1)
            dve.wait_ge(fs_pe, 4)
            nc.vector.tensor_copy(u1T[:, :], SC[0:VB, 0, 0:NSLOT]).then_inc(fs_ev, 1)
            dve.wait_ge(fs_hi, 1)
            nc.vector.tensor_tensor(ul[:, :, :], fwu1T[:, :, :], uh[:, :, :], ALU.subtract).then_inc(fs_lo, 1)
            for c in range(CC):
                dve.wait_ge(fs_hi, c + 2)
                nc.vector.tensor_tensor(al[:, c, :], PJ[:, c % 2, 0:2 * NSLOT], ah[:, c, :],
                                        ALU.subtract).then_inc(fs_lo, 1)
            dve.wait_ge(fs_hi, 6)
            nc.vector.tensor_tensor(v2l[:, :], PV[:, :], v2h[:, :], ALU.subtract).then_inc(fs_lo, 1)

            def statistics(k):
                dve.wait_ge(ln_m, NT * (k + 1))
                for n in range(NT):
                    ins = nc.vector.bn_aggr(mv[:, n, :], st[:, n, :])
                link(ins)
                nc.vector.tensor_scalar_add(ve[:, :], mv[:, :, 1], EPS).then_inc(ln_v, 1)
                dve.wait_ge(ln_sd, k + 1)
                link(nc.vector.reciprocal(rstd[:, :], sd[:, :]))
                link(nc.vector.tensor_tensor(nw[:, :], rstd[:, :], rstd[:, :], ALU.mult))
                link(nc.vector.tensor_tensor(nw[:, :], nw[:, :], ve[:, :], ALU.mult))
                link(nc.vector.tensor_scalar(nw[:, :], nw[:, :], -0.5, 1.5, ALU.mult, ALU.add))
                link(nc.vector.tensor_tensor(rstd[:, :], rstd[:, :], nw[:, :], ALU.mult))

            def layernorm(k):
                statistics(k)

                def normal(n, i):
                    xt = X[:, bass.ds(n, 1), :].rearrange("p a c -> p (a c)")
                    nc.vector.tensor_scalar(hbuf[:, i, :], xt, mv[:, bass.ds(n, 1), 0], rstd[:, bass.ds(n, 1)],
                                            ALU.subtract, ALU.mult).then_inc(ln_h, 1)

                def low(m, i):
                    dve.wait_ge(ln_hi, NT * k + 4 * m + i + 1)
                    cols = bass.ds(m * 4 * P + i * P, P)
                    nc.vector.tensor_tensor(XTl[:, :, cols], turn_bank(i).rearrange("p (c t) -> p c t", c=CC),
                                            XTh[:, :, cols], ALU.subtract).then_inc(ln_lo, 1)
                for n in range(3):
                    normal(n, n)
                with dve.Fori(0, NT // 4 - 1) as m:
                    for i in range(4):
                        normal(m * 4 + i + 3, (i + 3) % 4)
                        low(m, i)
                normal(NT - 1, 3)
                for i in range(4):
                    low(NT // 4 - 1, i)

            def ffn(f):
                k = 2 * f
                statistics(k)
                nc.vector.tensor_scalar(xa[:, :], rstd[:, :], 0.5, 1.0, ALU.mult, ALU.add)
                nc.vector.scalar_tensor_tensor(out=xb[:, :], in0=mv[:, :, 0], scalar=-0.5, in1=rstd[:, :],
                                               op0=ALU.mult, op1=ALU.mult).then_inc(x_ab, 1)

                def normal(n):
                    nc.vector.tensor_scalar(hbuf[:, n % 2, :], X[:, n, :], mv[:, n, 0:1], rstd[:, n:n + 1],
                                            ALU.subtract, ALU.mult).then_inc(ln_h, 1)

                def route(c, step):
                    a4 = asc[:, 4 * c:4 * c + 4, :]
                    if step < 2:
                        bank = score_bank(c, step).rearrange("p (t n) -> p t n", t=2)
                        lr2 = lrb[:, :].unsqueeze(1).to_broadcast([P, 2, NSLOT])
                        ts = slice(2 * step, 2 * step + 2)
                        dve.wait_ge(r_sc, 8 * f + 2 * c + step + 1)
                        nc.vector.scalar_tensor_tensor(out=rsc[:, ts, :], in0=bank[:, :, 0:NSLOT],
                                                       scalar=RDIM ** -0.5, in1=lr2, op0=ALU.mult, op1=ALU.add)
                        nc.vector.scalar_tensor_tensor(out=a4[:, ts, :], in0=bank[:, :, NSLOT:2 * NSLOT],
                                                       scalar=-BOT ** -0.5, in1=lr2, op0=ALU.mult,
                                                       op1=ALU.subtract).then_inc(r_use, 1)
                    if step == 2:
                        dve.wait_ge(r_use, 8 * f + 2 * c + 2)
                        for i in range(TB):
                            ins = nc.vector.max(m8[:, i, :], rsc[:, i, :])
                        link(ins)
                    if step == 3:
                        if c >= 2:
                            dve.wait_ge(r_am, 4 * f + c - 1)
                        for i in range(TB):
                            ins = nc.vector.match_replace(mr[:, c % 2, i, :], m8[:, i, :], rsc[:, i, :], SELECTED)
                        link(ins)
                        nc.vector.tensor_scalar(mr[:, c % 2, :, :], mr[:, c % 2, :, :], 0.99 * SELECTED, MASKED,
                                                ALU.is_gt, ALU.mult).then_inc(r_pen, 1)

                def minima(c):
                    dve.wait_ge(r_am, 4 * f + c + 1)
                    nc.vector.tensor_reduce(mnr[:, 4 * c:4 * c + 4], asc[:, 4 * c:4 * c + 4, :], AX_X,
                                            ALU.min).then_inc(r_mn, 1)

                normal(0)
                for c in range(6):
                    for i in range(4):
                        n = 4 * c + i
                        if n < NT - 1:
                            normal(n + 1)
                        if c >= 2:
                            route(c - 2, i)
                        if n < NT:
                            dve.wait_ge(ln_hi, NT * k + n + 1)
                            nc.vector.tensor_tensor(XTl[:, :, n * P:(n + 1) * P],
                                                    TR[:, n % 2, :].rearrange("p (c t) -> p c t", c=CC),
                                                    XTh[:, :, n * P:(n + 1) * P], ALU.subtract).then_inc(ln_lo, 1)
                    if c == 0:
                        link(nc.vector.reciprocal(gt2[:, :], ve[:, :]))
                        nc.vector.tensor_tensor(gt[:, :], mv[:, :, 1], gt2[:, :], ALU.mult).then_inc(g_lv, 1)
                    if c >= 3:
                        minima(c - 3)
                dve.wait_ge(g_lv, 2 * f + 2)
                nc.vector.reduce_sum(lsum[:, :], lv[:, :], AX_X).then_inc(g_sum, 1)
                minima(3)
                dve.wait_ge(g_ps, f + 1)
                link(nc.vector.tensor_scalar(lsum[:, :], PV[:, NT:NT + 1], 1.0 / (B * T), 1e-6, ALU.mult, ALU.add))
                link(nc.vector.reciprocal(lsum[:, :], lsum[:, :]))
                link(nc.vector.tensor_scalar(gt3[:, :], lv[:, :], lsum[:, 0:1], 0.5, ALU.mult, ALU.mult))

                def sigmoid_from(j):
                    nc.vector.tensor_scalar_max(gt[:, :], gt[:, :], -80.0).then_inc(g_ex, 1)
                    dve.wait_ge(g_exd, 2 * f + j + 1)
                    link(nc.vector.tensor_scalar_add(gt2[:, :], gt2[:, :], 1.0))
                    link(nc.vector.reciprocal(gt2[:, :], gt2[:, :]))

                link(nc.vector.tensor_scalar(gt[:, :], PV[:, 0:NT], bu2[:, 0:1], None, ALU.add))
                sigmoid_from(0)
                link(nc.vector.scalar_tensor_tensor(out=gt3[:, :], in0=gt2[:, :], scalar=2.5, in1=gt3[:, :],
                                                    op0=ALU.mult, op1=ALU.add))
                link(nc.vector.tensor_scalar(gt3[:, :], gt3[:, :], 0.0, 5.0, ALU.max, ALU.min))
                link(nc.vector.tensor_scalar(gt3[:, :], gt3[:, :], -TAU_LOW, 1.0 / (TAU_HIGH - TAU_LOW),
                                             ALU.add, ALU.mult))
                link(nc.vector.tensor_scalar(gt3[:, :], gt3[:, :], 0.0, 1.0, ALU.max, ALU.min))
                link(nc.vector.tensor_scalar(gt[:, :], gt3[:, :], gw[:, 0:1], gb[:, 0:1], ALU.mult, ALU.add))
                sigmoid_from(1)
                link(nc.vector.tensor_scalar(gt3[:, :], gt2[:, :], EARLY_EXIT, 0.5, ALU.is_ge, ALU.mult))
                link(nc.vector.tensor_tensor(gate[:, :], gt2[:, :], gt3[:, :], ALU.mult))

                dve.wait_ge(x_up, NT * (f + 1))

                def low(c):
                    c4 = slice(4 * c, 4 * c + 4)
                    dve.wait_ge(r_e, 4 * f + c + 1)
                    link(nc.vector.reciprocal(sm[:, c4], sm[:, c4]))
                    nc.vector.tensor_tensor(gs[:, c4], sm[:, c4], gate[:, c4], ALU.mult).then_inc(r_gs, 1)
                    dve.wait_ge(r_hi, 4 * f + c + 1)
                    nc.vector.tensor_tensor(eTl[:, c % 2, :], TR[:, c % 2, :], eTh[:, c % 2, :],
                                            ALU.subtract).then_inc(r_lo, 1)

                def next_moments(c):
                    if f == 0:
                        dve.wait_ge(r_xd, 2 * c + 2)
                        dve.wait_ge(r_xp, 2 * c + 2)
                        for n in range(4 * c, 4 * c + 4):
                            moments(n)
                low(0)
                for c in range(4):
                    if c < 3:
                        low(c + 1)
                    if c == 0:
                        dve.wait_ge(r_gs, 4 * f + 1)
                    for n in (4 * c, 4 * c + 2):
                        dve.wait_ge(r_aux, NT * f + n + 1)
                        nc.vector.scalar_tensor_tensor(out=X[:, n, :], in0=SC[:, 2, :], scalar=gs[:, n:n + 1],
                                                       in1=X[:, n, :], op0=ALU.mult, op1=ALU.add).then_inc(r_xd, 1)
                    if c:
                        next_moments(c - 1)
                next_moments(3)
                dve.wait_ge(r_xd, 8 * f + 8)
                dve.wait_ge(r_xp, 8 * f + 8)

            ffn(0)
            layernorm(1)

            dve.wait_ge(bo_add, NT)
            dve.wait_ge(ld_t, 80)

            def rope(kind, n, idx, n0, bank):
                r = rope_index(kind, n, idx, n0)
                r0 = rope_index(kind, n0, idx, n0)
                j, (c_, s_) = r0 % NROPE, ((cq, sq) if kind == "Q" else (ck, sk))
                if kind == "Q":
                    dve.wait_ge(s_q, 4 * n + idx + 1)
                else:
                    dve.wait_ge(s_k, n + 1)
                if r0 >= NROPE:
                    dve.wait_ge(rope_lo, r - NROPE + 1)
                H = P // 2
                nc.vector.tensor_tensor(t1[:, j, :], PJ[:, bank, :], c_[:, :], ALU.mult)
                nc.vector.tensor_tensor(t2[0:H, j, :], PJ[H:P, bank, :], s_[0:H, :], ALU.mult)
                nc.vector.tensor_tensor(t2[H:P, j, :], PJ[0:H, bank, :], s_[H:P, :], ALU.mult).then_inc(rope_mul, 1)

            def value_lo(n, n0, bank):
                dve.wait_ge(v_hi, n + 1)
                nc.vector.tensor_tensor(vl[:, n0 % 2, :, :], PJ[:, bank, :].rearrange("p (a d) -> p a d", a=TB),
                                        vh[:, n0 % 2, :, :], ALU.subtract).then_inc(v_lo, 1)

            def project_add(n, i, b, bank):
                dve.wait_ge(s_o, 4 * n + i + 1)
                xt = X[:, TB * b + i, :]
                nc.vector.tensor_tensor(xt, PJ[:, bank, :], xt, ALU.add).then_inc(o_add, 1)

            def p_lo(s, j):
                dve.wait_ge(tr_hi, 4 * s + j + 1)
                w = (TB - j) * P
                nc.vector.tensor_tensor(pTl[:, TOFF[j]:TOFF[j] + w], TR[:, j % 2, 0:w], pTh[:, TOFF[j]:TOFF[j] + w],
                                        ALU.subtract).then_inc(tr_lo, 1)

            def out_lo(s, b, h):
                dve.wait_ge(o_hi, s + 1)
                nc.vector.scalar_tensor_tensor(out=oTl[:, b % 2, h, :], in0=PV[:, :], scalar=1.0 / PSCALE,
                                               in1=oTh[:, b % 2, h, :], op0=ALU.mult,
                                               op1=ALU.subtract).then_inc(o_lo, 1)

            for kind, n, idx, bank in PROLOGUE:
                if kind in "QK":
                    rope(kind, n, idx, n, bank)
                if kind == "V":
                    value_lo(n, n, bank)

            d_rec = sem("d_rec")

            def body(g, first, last):
                g0 = rep(g, first, last)
                for b in range(B):
                    for h in range(HG):
                        n, n0 = B * g + b, B * g0 + b
                        s = 4 * n + h
                        prev = not (first and b == 0 and h == 0)
                        pb_, ph_ = ((b - 1) % B if h == 0 else b), (h - 1) % HG
                        if prev:
                            p_lo(s - 1, 0)
                            p_lo(s - 1, 1)
                        for k, tiles in enumerate(SBANKS):
                            dve.wait_ge(s_sc, 3 * s + k + 1)
                            for i in tiles:
                                w = (i + 1) * P
                                ins = nc.vector.tensor_reduce(mn[:, h % 2, i:i + 1], SCf[:, SOFF[i]:SOFF[i] + w],
                                                              AX_X, ALU.min)
                            ins.then_inc(d_min, 1)
                        if prev:
                            p_lo(s - 1, 2)
                            p_lo(s - 1, 3)
                        dve.wait_ge(a_exp, 3 * s + 3)
                        nc.vector.reciprocal(ri[:, h % 2, :], rs[:, h % 2, :]).then_inc(d_rec, 1)
                        dve.wait_ge(d_rec, s + 1)
                        for i in range(TB - 1, -1, -1):
                            pt = p[:, h % 2, SOFF[i]:SOFF[i] + (i + 1) * P]
                            ins = nc.vector.tensor_scalar(pt, pt, ri[:, h % 2, i:i + 1], PSCALE, ALU.mult, ALU.mult)
                        ins.then_inc(d_norm, 1)
                        qs, rest = tasks_of(n0, h)
                        for kind, m0, idx, bank in qs:
                            rope(kind, n + (m0 - n0), idx, m0, bank)
                        if prev:
                            out_lo(s - 1, pb_, ph_)
                        for kind, m0, idx, bank in rest:
                            m = n + (m0 - n0)
                            if kind == "K":
                                rope(kind, m, idx, m0, bank)
                            if kind == "V":
                                value_lo(m, m0, bank)
                            if kind == "O":
                                project_add(m, idx, m0 % B, bank)
                                if m0 >= (G - 1) * B:
                                    dve.wait_ge(o_add, 4 * m + idx + 1)
                                    moments(TB * (m0 % B) + idx)
            bodies(dve, body)
            SL = G * B * HG
            for j in range(TB):
                p_lo(SL - 1, j)
            out_lo(SL - 1, B - 1, HG - 1)
            for kind, n, idx, bank in EPILOGUE:
                project_add(n, idx, n % B, bank)
                dve.wait_ge(o_add, 4 * n + idx + 1)
                moments(TB * (n % B) + idx)
            dve.wait_ge(o_add, 4 * G * B)

            ffn(1)

        @block.tensor
        def _(pe):
            mm = nc.tensor.matmul

            def mm3(out_, lh, ll, rh, rl, start, stop):
                mm(out_, lh, rh, start=start, stop=False)
                mm(out_, lh, rl, start=False, stop=False)
                return mm(out_, ll, rh, start=False, stop=stop)

            pe.wait_ge(ld_f, 16 * NFL)
            mm(PV[0:RDIM, 0:NSLOT], fwrT[:, :], fkeyT[:, :], start=True, stop=True).then_inc(fs_pe, 1)
            pe.wait_ge(fs_ev, 1)
            mm(TR[0:BOT, 0, 0:NSLOT], fwr[:, :], rk[:, :], start=True, stop=True).then_inc(fs_pe, 1)
            for c in range(CC):
                ins = mm(SC[0:VB, 0, 0:NSLOT], fwvdT[:, c, :], fvalT[:, c, :], start=c == 0, stop=c == CC - 1)
            ins.then_inc(fs_pe, 2)
            pe.wait_ge(fs_ev, 2)
            for c in range(CC):
                if c >= 2:
                    pe.wait_ge(fs_lo, c)
                mm(PJ[:, c % 2, 0:NSLOT], fwq[:, c * P:(c + 1) * P], rmat[:, :], start=True, stop=True)
                mm(PJ[:, c % 2, NSLOT:2 * NSLOT], fwq[:, c * P:(c + 1) * P], fkeyT[:, :],
                   start=True, stop=True).then_inc(fs_pe, 1)
            pe.wait_ge(fs_ev, 3)
            mm(PV[:, :], u1T[:, :], fwvuT[:, :], start=True, stop=True).then_inc(fs_pe, 1)
            pe.wait_ge(cst, 1)

            def layernorm(k):
                with pe.Fori(0, NT // 4) as m:
                    for i in range(4):
                        pe.wait_ge(ln_h, NT * k + 4 * m + i + 1)
                        pe.wait_ge(ln_lo, NT * k + 4 * m + i - 3)
                        for c in range(CC):
                            ins = nc.tensor.transpose(turn_bank(i)[:, c * P:(c + 1) * P],
                                                      hbuf[:, i, c * P:(c + 1) * P], ident[:, :])
                        ins.then_inc(ln_t, 1)

            def ffn(f):
                k = 2 * f
                if f:
                    pe.wait_ge(o_add, 4 * G * B)

                def hidden(c, j):
                    if c >= 1 and j == 0:
                        pe.wait_ge(u_g, 4 * f + c)
                    xs = slice(c * T, (c + 1) * T)
                    ins = mm3(PJ[:, 0, :], uh[:, j, :], ul[:, j, :], XTh[:, j, xs], XTl[:, j, xs],
                              j == 0, j == CC - 1)
                    if j == CC - 1:
                        ins.then_inc(u_ps, 1)

                def hidden_out(c):
                    pe.wait_ge(u_g, 4 * f + c + 1)
                    for i in range(TB):
                        n = 4 * c + i
                        ins = mm(PV[:, n:n + 1], gT[:, c % 2, i * P:(i + 1) * P], wu2T[:, :], start=True, stop=True)
                    ins.then_inc(u_l, 1)

                def score(c, i):
                    if c >= 2 and i == 0:
                        pe.wait_ge(r_use, 8 * f + 2 * (c - 2) + 2)
                    n = 4 * c + i
                    bank = score_bank(c, i // 2)[:, (i % 2) * 2 * NSLOT:(i % 2 + 1) * 2 * NSLOT]
                    for j in range(CC):
                        xs = slice(n * P, (n + 1) * P)
                        ins = mm3(bank, XTh[:, j, xs], XTl[:, j, xs], ah[:, j, :], al[:, j, :],
                                  j == 0, j == CC - 1)
                    if i % 2:
                        ins.then_inc(r_sc, 1)

                for c in range(5):
                    for i in range(4):
                        n = 4 * c + i
                        if c < 4:
                            pe.wait_ge(ln_h, NT * k + n + 1)
                            if n >= 2:
                                pe.wait_ge(ln_lo, NT * k + n - 1)
                            for j in range(CC):
                                ins = nc.tensor.transpose(TR[:, n % 2, j * P:(j + 1) * P],
                                                          hbuf[:, n % 2, j * P:(j + 1) * P], ident[:, :])
                            ins.then_inc(ln_t, 1)
                        if c and i == 0:
                            if c == 1:
                                pe.wait_ge(fs_lo, 6)
                            pe.wait_ge(ln_lo, NT * k + 4 * c)
                        if c:
                            score(c - 1, i)
                            hidden(c - 1, i)
                        if c >= 2 and i == 3:
                            hidden_out(c - 2)
                hidden_out(3)
                pe.wait_ge(g_sum, f + 1)
                mm(PV[:, NT:NT + 1], ones[:, :], lsum[:, :], start=True, stop=True).then_inc(g_ps, 1)

                def turn(c):
                    pe.wait_ge(r_e, 4 * f + c + 1)
                    for i in range(TB):
                        ins = nc.tensor.transpose(TR[:, c % 2, i * P:(i + 1) * P], asc[:, 4 * c + i, :], ident[:, :])
                    ins.then_inc(r_t, 1)
                turn(0)
                for c in range(4):
                    if c < 3:
                        turn(c + 1)
                    pe.wait_ge(r_lo, 4 * f + c + 1)
                    for i in range(TB):
                        n = 4 * c + i
                        if n >= 2:
                            pe.wait_ge(*((r_xa, 8 * f + n // 2) if n % 2 else (r_xd, 8 * f + n // 2)))
                        ts = slice(i * P, (i + 1) * P)
                        mm3(PJ[:, 0, :] if n % 2 else SC[:, 2, :], eTh[:, c % 2, ts], eTl[:, c % 2, ts],
                            v2h[:, :], v2l[:, :], True, True).then_inc(r_aux, 1)

            ffn(0)
            layernorm(1)

            def proj(kind, n, idx, n0, bank):
                b, g0 = n0 % B, n0 // B
                g = (n - b) // B if isinstance(n, int) else None
                before = BEFORE[(kind, n0, idx)]
                if before:
                    bk, bn, bi, _ = before
                    pe.wait_ge(*consumed(bk, n + (bn - n0), bi, bn))
                if kind in "QKV":
                    k = PIECES.index(kind + (str(idx) if kind == "Q" else ""))
                    return b, k
                return b, None

            def project(kind, n, idx, n0, bank, g):
                b, k = proj(kind, n, idx, n0, bank)
                xs = slice(b * T, (b + 1) * T)
                out_ = PJ[:, bank, :]
                if kind in "QK":
                    pe.wait_ge(w_lo, NPC * g + k + 1)
                    for c in range(CC):
                        ins = mm3(out_, wh[:, k, c, :], wl[:, k, c, :], XTh[:, c, xs], XTl[:, c, xs],
                                  c == 0, c == CC - 1)
                    ins.then_inc(s_q if kind == "Q" else s_k, 1)
                elif kind == "V":
                    pe.wait_ge(w_lo, NPC * g + k + 1)
                    for t in range(TB):
                        ts = slice(b * T + t * P, b * T + (t + 1) * P)
                        for c in range(CC):
                            ins = mm3(out_[:, t * D:(t + 1) * D], XTh[:, c, ts], XTl[:, c, ts],
                                      wh[:, k, c, :], wl[:, k, c, :], c == 0, c == CC - 1)
                    ins.then_inc(s_v, 1)
                else:
                    if idx == 0:
                        pe.wait_ge(o_lo, 4 * n + 4)
                        pe.wait_ge(wo_lo, HG * g + HG)
                    ts = slice(idx * P, (idx + 1) * P)
                    for h in range(HG):
                        ins = mm3(out_, oTh[:, b % 2, h, ts], oTl[:, b % 2, h, ts], woh[:, h, :], wol[:, h, :],
                                  h == 0, h == HG - 1)
                    ins.then_inc(s_o, 1)

            def transposed(s, s0, j):
                if j == 0:
                    pe.wait_ge(d_norm, s + 1)
                if s0 > 0 or j >= 2:
                    pe.wait_ge(tr_lo, 4 * s + j - 1)
                else:
                    pe.wait_ge(ln_lo, 2 * NT)
                for i in range(j, TB):
                    ins = nc.tensor.transpose(TR[:, j % 2, (i - j) * P:(i - j + 1) * P],
                                              p[:, s0 % 2, SOFF[i] + j * P:SOFF[i] + (j + 1) * P], ident[:, :])
                ins.then_inc(s_tr, 1)

            def attend(s, s0, j):
                pe.wait_ge(tr_lo, 4 * s + j + 1)
                if j == 0:
                    if s0 > 0:
                        pe.wait_ge(o_lo, s)
                par = (s0 // 4) % 2
                w = (TB - j) * P
                ins = mm3(PV[:, j * P:T], vh[:, par, j, :], vl[:, par, j, :], pTh[:, TOFF[j]:TOFF[j] + w],
                          pTl[:, TOFF[j]:TOFF[j] + w], j == 0, j == TB - 1)
                if j == TB - 1:
                    ins.then_inc(s_pv, 1)

            def scores(s, s0, n, n0, h):
                pe.wait_ge(rope_lo, rope_index("Q", n, h, n0) + 1)
                for k, tiles in enumerate(SBANKS):
                    if s0 > 0:
                        pe.wait_ge(a_exp, 3 * s + k - 2)
                    for i in tiles:
                        w = (i + 1) * P
                        ts = slice(i * P, w)
                        o = SCf[:, SOFF[i]:SOFF[i] + w]
                        qh, ql, kh, kl = (qTh[:, h, ts], qTl[:, h, ts], kTh[:, n0 % 2, 0:w], kTl[:, n0 % 2, 0:w])
                        mm(o, qh, kh, start=True, stop=False)
                        mm(o, qh, kl, start=False, stop=False)
                        mm(o, ql, kh, start=False, stop=False)
                        ins = mm(SCf[:, SOFF[i] + w - P:SOFF[i] + w], identb[:, :], maskb[:, :],
                                 start=False, stop=True)
                    ins.then_inc(s_sc, 1)

            pe.wait_ge(ln_lo, 2 * NT)
            for kind, n, idx, bank in PROLOGUE:
                if kind == "V":
                    pass
                project(kind, n, idx, n, bank, 0)
            pe.wait_ge(v_lo, 1)

            def body(g, first, last):
                g0 = rep(g, first, last)
                for b in range(B):
                    for h in range(HG):
                        n, n0 = B * g + b, B * g0 + b
                        s, s0 = 4 * n + h, 4 * n0 + h
                        prev = s0 > 0

                        def run(tasks):
                            for kind, m0, idx, bank in tasks:
                                project(kind, n + (m0 - n0), idx, m0, bank, g + (m0 // B - g0))
                        if prev:
                            transposed(s - 1, s0 - 1, 0)
                            transposed(s - 1, s0 - 1, 1)
                        scores(s, s0, n, n0, h)
                        if prev:
                            if h == 1:
                                pe.wait_ge(v_lo, n + 1)
                            attend(s - 1, s0 - 1, 0)
                            transposed(s - 1, s0 - 1, 2)
                            attend(s - 1, s0 - 1, 1)
                            transposed(s - 1, s0 - 1, 3)
                        qs, rest = tasks_of(n0, h)
                        run(qs)
                        if prev:
                            attend(s - 1, s0 - 1, 2)
                            attend(s - 1, s0 - 1, 3)
                        run(rest)
            bodies(pe, body)
            SL = G * B * HG
            transposed(SL - 1, SL - 1, 0)
            transposed(SL - 1, SL - 1, 1)
            attend(SL - 1, SL - 1, 0)
            transposed(SL - 1, SL - 1, 2)
            attend(SL - 1, SL - 1, 1)
            transposed(SL - 1, SL - 1, 3)
            attend(SL - 1, SL - 1, 2)
            attend(SL - 1, SL - 1, 3)
            for kind, n, idx, bank in EPILOGUE:
                project(kind, n, idx, n, bank, G - 1)

            ffn(1)


NROPE = 4
NFL = 14
SPLIT_AT = {(2, 1): [0], (2, 3): [1], (3, 0): [2, 3], (3, 1): [4], (3, 2): [5]}


def kernel(**inputs):
    import numpy as np
    import concourse.bacc as bacc
    from concourse.bass_utils import run_bass_kernel_spmd

    a = {k: np.asarray(v) for k, v in inputs.items()}
    perm = np.concatenate([np.arange(0, D, 2), np.arange(1, D, 2)])
    wq = a["L0_attn_Wq"].reshape(CC, P, G, HG, D)[..., perm].transpose(2, 1, 3, 0, 4)
    wk = a["L0_attn_Wk"].reshape(CC, P, G, D)[..., perm].transpose(2, 1, 0, 3)
    wv = a["L0_attn_Wv"].reshape(CC, P, G, D).transpose(2, 1, 0, 3)
    parts = {"K": wk, "V": wv, **{f"Q{h}": wq[:, :, h] for h in range(HG)}}
    wqkv = np.stack([parts[k] for k in PIECES], axis=2)
    wo = a["L0_attn_Wo"].reshape(G, HG, D, C).transpose(0, 2, 1, 3)
    freqs = (1.0 / np.float32(10000.0) ** (np.arange(0, D, 2, dtype=np.float32) / np.float32(D))).astype(np.float32)
    angle = np.arange(T, dtype=np.float32)[None, :] * freqs[:, None]
    cos, sin = np.cos(angle), np.sin(angle)
    cosk, sink = np.concatenate([cos, cos]), np.concatenate([-sin, sin])
    arrays = {
        "x": a["L0_attn_x"].reshape(B * T, C), "wqkv": wqkv, "wo": wo, "bo": a["L0_attn_bo"].reshape(1, C),
        "cosq": cosk * np.float32(-SCALE), "sinq": sink * np.float32(-SCALE), "cosk": cosk, "sink": sink,
        "f_wq": a["L0_ffn_Wq"], "f_wr": a["L0_ffn_Wr"], "f_wrT": a["L0_ffn_Wr"].T,
        "f_keyT": a["L0_ffn_aux_keys"].T, "f_valT": a["L0_ffn_aux_values"].T, "f_wvdT": a["L0_ffn_Wvd"].T,
        "f_wvuT": a["L0_ffn_Wvu"].T, "f_wu1T": a["L0_ffn_Wu1"].T, "f_bu1": a["L0_ffn_bu1"].reshape(P, 1),
        "f_wu2T": a["L0_ffn_Wu2"].T, "f_bu2": a["L0_ffn_bu2"].reshape(1, 1),
        "f_gw": a["L0_ffn_gate_w1"].reshape(1, 1), "f_gb": a["L0_ffn_gate_bias"].reshape(1, 1),
        "f_lr": a["L0_ffn_log_rel"].reshape(1, NSLOT),
    }
    arrays = {k: np.ascontiguousarray(v) for k, v in arrays.items()}
    nc = bacc.Bacc("TRN2", target_bir_lowering=False, num_devices=1)
    args = [nc.dram_tensor(f"in_{k}", v.shape, mybir.dt.from_np(v.dtype), kind="ExternalInput").ap()
            for k, v in arrays.items()]
    out = nc.dram_tensor("out_0", (B * T, C), F32, kind="ExternalOutput").ap()
    macaron_kernel(nc, *args, out)
    r = run_bass_kernel_spmd(nc, [{f"in_{k}": v for k, v in arrays.items()}], core_ids=[0])
    return r.results[0]["out_0"].reshape(B, T, C)
```
